# Optimizing a Trainium2 kernel written in Bass

```python
import numpy as np
import jax
import jax.numpy as jnp

def _softmax(x, axis=-1):
    return jax.nn.softmax(x, axis=axis)

def _gelu(x):
    return jax.nn.gelu(x, approximate=True)

def _silu(x):
    return jax.nn.silu(x)

def _sigmoid(x):
    return jax.nn.sigmoid(x)

def _layernorm(x, axis=-1, eps=1e-05):
    m = jnp.mean(x, axis=axis, keepdims=True)
    v = jnp.var(x, axis=axis, keepdims=True)
    return (x - m) / jnp.sqrt(v + eps)

def _scatter_add(tgt, idx, src, axis=0):
    return tgt.at[idx].add(src)

def _segment_sum(src, seg, n):
    return jax.ops.segment_sum(src, seg, n)
kernel_name = 'mk_conv_preact_d1_conv_nchw384_r2_6287c4'

def setup_inputs(seed: int=0):
    np.random.seed(seed)
    _w = jnp.asarray

    def _rec_inputs():
        import jax
        import jax.numpy as jnp
        _gk = jax.random.key(seed)
        x = -0.0001538 + 1 * jax.random.normal(jax.random.fold_in(_gk, 1), (16, 192, 32, 32), jnp.float32)
        return x
    x = _rec_inputs()

    def _L0_conv_setup():
        import jax, jax.numpy as jnp
        import numpy as np
        DIM = 192
        DIM_HEAD = 32
        NUM_HEAD = DIM // DIM_HEAD
        SCALE = DIM_HEAD ** (-0.5)
        key = jax.random.key(seed)
        k1, k2, k3, k4 = jax.random.split(key, 4)
        x = jax.random.normal(k1, (16, DIM, 32, 32), dtype=jnp.float32)
        qkv_w = jax.random.normal(k2, (3 * DIM, DIM), dtype=jnp.float32) * DIM ** (-0.5)
        proj_w = jax.random.normal(k3, (DIM, DIM), dtype=jnp.float32) * DIM ** (-0.5)
        proj_b = jax.random.normal(k4, (DIM,), dtype=jnp.float32) * 0.01
        return {'x': x, 'qkv_w': qkv_w, 'proj_w': proj_w, 'proj_b': proj_b}
    _L0_conv_all = _L0_conv_setup()
    _L0_conv_in = {k: v for k, v in _L0_conv_all.items() if k in ('qkv_w', 'proj_w', 'proj_b')}
    del _L0_conv_all
    return {'x': x, 'L0_conv_qkv_w': _L0_conv_in['qkv_w'], 'L0_conv_proj_w': _L0_conv_in['proj_w'], 'L0_conv_proj_b': _L0_conv_in['proj_b']}

def reference(x, L0_conv_qkv_w, L0_conv_proj_w, L0_conv_proj_b):
    import jax
    import jax.numpy as jnp

    def _L0_conv_ref(x, qkv_w, proj_w, proj_b):
        import jax, jax.numpy as jnp
        import numpy as np
        DIM = 192
        DIM_HEAD = 32
        NUM_HEAD = DIM // DIM_HEAD
        SCALE = DIM_HEAD ** (-0.5)
        B, C, H, W = x.shape
        N = H * W
        xt = x.reshape(B, C, N).transpose(0, 2, 1)
        qkv = jnp.einsum('bnc,oc->bno', xt, qkv_w)
        qkv = qkv.reshape(B, N, 3, NUM_HEAD, DIM_HEAD).transpose(2, 0, 3, 1, 4)
        q, k, v = (qkv[0], qkv[1], qkv[2])
        attn = jnp.einsum('bhnd,bhmd->bhnm', q, k) * SCALE
        attn = jax.nn.softmax(attn, axis=-1)
        out = jnp.einsum('bhnm,bhmd->bhnd', attn, v)
        out = out.transpose(0, 2, 1, 3).reshape(B, N, C)
        out = jnp.einsum('bnc,oc->bno', out, proj_w) + proj_b
        return out.transpose(0, 2, 1).reshape(B, C, H, W)

    def _gn(v, G=32, eps=1e-05):
        B_, C_, H_, W_ = v.shape
        g = v.reshape(B_, G, C_ // G, H_, W_)
        m = jnp.mean(g, axis=(2, 3, 4), keepdims=True)
        s = jnp.var(g, axis=(2, 3, 4), keepdims=True)
        return ((g - m) / jnp.sqrt(s + eps)).reshape(v.shape)

    def _ln_c(v, eps=1e-06):
        m = jnp.mean(v, axis=1, keepdims=True)
        s = jnp.var(v, axis=1, keepdims=True)
        return (v - m) / jnp.sqrt(s + eps)

    def _ln_t(v, eps=1e-05):
        m = jnp.mean(v, axis=-1, keepdims=True)
        s = jnp.var(v, axis=-1, keepdims=True)
        return (v - m) / jnp.sqrt(s + eps)

    def _to_tokens(v):
        B_, C_, H_, W_ = v.shape
        return v.reshape(B_, C_, H_ * W_).transpose(0, 2, 1)

    def _from_tokens(t, like):
        B_, C_, H_, W_ = like.shape
        return t.transpose(0, 2, 1).reshape(B_, C_, H_, W_)
    x = x + _L0_conv_ref(_gn(x), L0_conv_qkv_w, L0_conv_proj_w, L0_conv_proj_b)
    return x

_drawn_inputs = setup_inputs


def setup_inputs(seed=0):
    import zlib

    import numpy as np

    out = dict(_drawn_inputs(seed))
    spreads = {}
    factors = {'L0_conv_proj_b': 6.007}
    for name, (base, spread) in spreads.items():
        noise = np.random.default_rng([zlib.crc32(name.encode()), seed]).standard_normal(out[name].shape)
        drawn = base * np.exp(spread * noise) if base else spread * noise
        out[name] = jnp.asarray(drawn.astype(out[name].dtype))
    for name, factor in factors.items():
        out[name] = (out[name] * factor).astype(out[name].dtype)
    return out
```

```python
from contextlib import ExitStack
from math import sqrt

import numpy as np

import concourse.bass as bass
from concourse import mybir

F32 = mybir.dt.float32
F16 = mybir.dt.float16
ALU = mybir.AluOpType
ACT = mybir.ActivationFunctionType
AX_X = mybir.AxisListType.X

BATCH = 16
C = 192
H = W = 32
N = H * W
HEADS = 6
D = C // HEADS
GROUPS = 32
GROUP = C // GROUPS
EPS = 1e-5
SCALE = D ** -0.5

P = 128
HALF = 512
HALVES = N // HALF
TILES = N // P
PAIRS = HEADS // 2
SLOTS = PAIRS * TILES
CB = C - P
SCORE_UNITS = 4
SCORE_BANKS = 3
RING = 4
OM = C // 2

STACK = 3 * D
SHIFTED = STACK + 2
SHIFT = 2.0 ** 15
LIMIT = 8192.0
XHAT_MAX = sqrt(GROUP * N)

SHIFT_SLOTS = {1: 2, 9: 0, 17: 1}
MEAN_SLOT, VAR_SLOT = 2, 3
XHAT_SLOTS = (4, 5, 6, 7)
PROJ_SLOTS = (5, 6, 7, 8)
V_SLOTS = (10, 11, 12, 13)
QK_SLOTS = (14, 15, 16, 18, 19, 20)
NORM_SLOTS = {3: 2, 11: 0, 19: 1}
LOAD_SLOT = 8

STATS = 9
XHAT = 4
MOVE = 16
STACK_MOVES = 12


class Step:

    def __init__(self, b, at, misc, odd):
        self.b = b
        self.parity = at % 2
        self.attend = 0 <= at < BATCH
        self.shift_last = self.attend
        self.maxima = 0 <= at + 1 < BATCH
        self.project_in = 0 <= at + 2 < BATCH
        self.tail = 0 <= at - 1 < BATCH
        self.misc = misc
        self.odd = odd

    def uses(self):
        out = []
        for s in range(SLOTS):
            if self.maxima:
                out += [(s, "max", u) for u in range(SCORE_UNITS)]
            if s in SHIFT_SLOTS and (self.shift_last if SHIFT_SLOTS[s] == PAIRS - 1 else self.maxima):
                out.append((s, "shift", SHIFT_SLOTS[s]))
            if self.project_in and s == MEAN_SLOT:
                out.append((s, "mean", 0))
            if self.project_in and s == VAR_SLOT:
                out.append((s, "var", 0))
            if self.tail and s in PROJ_SLOTS:
                out.append((s, "proj", PROJ_SLOTS.index(s)))
            if self.maxima and s in V_SLOTS:
                out.append((s, "v", V_SLOTS.index(s)))
            if self.project_in and s in QK_SLOTS:
                out.append((s, "qk", QK_SLOTS.index(s)))
        return out

    def at_slot(self, s):
        return [(self.misc + n, (self.odd + n) % 2, kind, i)
                for n, (slot, kind, i) in enumerate(self.uses()) if slot == s]

    def ordinal(self, kind, index):
        return self.misc + [(k, i) for _, k, i in self.uses()].index((kind, index))


LOOP_FIRST, LOOP_END = 1, 13


def run_steps(eng, step):
    misc = 0
    for at in range(-2, LOOP_FIRST):
        st = Step(at, at, misc, misc % 2)
        step(st)
        misc += len(st.uses())
    per = len(Step(LOOP_FIRST, LOOP_FIRST, 0, 0).uses())
    with eng.Fori(0, (LOOP_END - LOOP_FIRST) // 2) as i:
        for k in range(2):
            step(Step(2 * i + (LOOP_FIRST + k), LOOP_FIRST + k, 2 * per * i + (misc + per * k),
                      (misc + per * k) % 2))
    misc += per * (LOOP_END - LOOP_FIRST)
    for at in range(LOOP_END, BATCH + 1):
        st = Step(at, at, misc, misc % 2)
        step(st)
        misc += len(st.uses())


def due(count):
    return not isinstance(count, int) or count > 0


def group_norm_attention(nc, x, qkv_wT, proj_wT, proj_b, group_mean, identity, out):
    with ExitStack() as ctx:
        def sb(name, shape, dt):
            return ctx.enter_context(nc.sbuf_tensor(name, shape, dt))

        def psum(name, shape):
            return ctx.enter_context(nc.psum_tensor(name, shape, F32))

        def sem(name):
            return ctx.enter_context(nc.semaphore(name))

        scores_ps = psum("scores_ps", [P, SCORE_BANKS, HALF])
        misc_ps = psum("misc_ps", [P, 2, HALF])
        heads_ps = psum("heads_ps", [P, 2, HALF])
        sums_ps = psum("sums_ps", [P, HALF])

        q_stack = sb("q_stack", [P, 2, HEADS, N], F16)
        k_stack = sb("k_stack", [P, 2, HEADS, N], F16)
        v_sb = sb("v_sb", [P, 2, TILES, C], F32)
        probs = sb("probs", [P, 2, RING, N], F32)
        prob_pairs = sb("prob_pairs", [P, 2, 2, N], F32)
        xhat_a_hi = sb("xhat_a_hi", [P, 2, N], F16)
        xhat_a_lo = sb("xhat_a_lo", [P, 2, N], F16)
        xhat_b = sb("xhat_b", [P, 2, N], F16)
        xhat = sb("xhat", [P, 2, N], F32)
        x_sb = sb("x_sb", [P, 2, N], F32)
        qk_hi = sb("qk_hi", [P, 3, N], F16)
        qk_lo = sb("qk_lo", [P, 3, N], F16)
        heads_out = sb("heads_out", [P, HALF], F32)
        sums_inv = sb("sums_inv", [P, HALF], F32)
        attn = sb("attn", [P, 2, N], F32)
        x_res = sb("x_res", [OM, 2, N], F32)
        y = sb("y", [OM, 2, N], F32)

        w_f32 = sb("w_f32", [P, 2, 3 * C], F32)
        w_hi = sb("w_hi", [P, 2, 3 * C], F16)
        w_lo = sb("w_lo", [P, 2, 3 * C], F16)
        wp = sb("wp", [P, 2, C], F32)
        bias = sb("bias", [OM, 2], F32)
        mean_a = sb("mean_a", [P, 2, P], F32)
        mean_b = sb("mean_b", [CB, 2, P], F32)
        ident = sb("ident", [P, P], F32)
        ones = sb("ones", [P, P], F32)
        ones_v = sb("ones_v", [P, D], F32)
        l1_max = sb("l1_max", [P, 3], F32)
        unscale = sb("unscale", [P, 3], F32)
        rescale = sb("rescale", [P, 3], F32)
        exp_scale = sb("exp_scale", [P, 1], F32)

        half_stats = sb("half_stats", [P, 2, HALVES, 6], F32)
        chan_stats = sb("chan_stats", [P, 2, 2], F32)
        neg_mu = sb("neg_mu", [P, 2], F32)
        mu_off = sb("mu_off", [P, 2], F32)
        mu_off2 = sb("mu_off2", [P, 2], F32)
        chan_var = sb("chan_var", [P, 2], F32)
        var_eps = sb("var_eps", [P, 2], F32)
        minus_half = sb("minus_half", [P, 2], F32)
        rstd = sb("rstd", [P, 2], F32)
        neg_mu_rstd = sb("neg_mu_rstd", [P, 2], F32)
        half_max = sb("half_max", [P, 2, TILES, HALVES], F32)
        neg_max = sb("neg_max", [P, 2 * TILES], F32)
        shift_rows = sb("shift_rows", [2 * TILES, 2, P], F16)

        const_loaded = sem("const_loaded")
        setup = sem("setup")
        l1_ready = sem("l1_ready")
        x_loaded = sem("x_loaded")
        stats_step = sem("stats_step")
        halves_seen = sem("halves_seen")
        rstd_step = sem("rstd_step")
        xhat_ready = sem("xhat_ready")
        xlo_ready = sem("xlo_ready")
        misc_filled = sem("misc_filled")
        misc_freed = sem("misc_freed")
        qk_hi_ready = sem("qk_hi_ready")
        stacked = [sem(f"stacked{p}") for p in range(PAIRS)]
        neg_max_ready = sem("neg_max_ready")
        shift_step = sem("shift_step")
        shift_moved = sem("shift_moved")
        scores_ready = sem("scores_ready")
        probs_ready = sem("probs_ready")
        pairs_added = sem("pairs_added")
        heads_done = sem("heads_done")
        sums_done = sem("sums_done")
        inverted = sem("inverted")
        norm_done = sem("norm_done")
        attn_moved = sem("attn_moved")
        res_loaded = sem("res_loaded")
        y_stored = sem("y_stored")

        block = ctx.enter_context(nc.Block())

        @block.sync
        def _(sp):
            sp.dma_start(w_f32[:, 0, :], qkv_wT[0:P, :]).then_inc(const_loaded, MOVE)
            for r in range(2):
                sp.dma_start(w_f32[CB * r:CB * (r + 1), 1, :], qkv_wT[P:C, :]).then_inc(const_loaded, MOVE)
            sp.dma_start(wp[:, 0, :], proj_wT[0:P, :]).then_inc(const_loaded, MOVE)
            sp.dma_start(wp[0:CB, 1, :], proj_wT[P:C, :]).then_inc(const_loaded, MOVE)
            sp.dma_start(bias[:, :], proj_b).then_inc(const_loaded, MOVE)
            sp.dma_start(ident[:, :], identity).then_inc(const_loaded, MOVE)
            sp.dma_start(mean_a[:, 0, :], group_mean[0:P, 0:P]).then_inc(const_loaded, MOVE)
            sp.dma_start(mean_b[:, 0, :], group_mean[P:C, 0:P]).then_inc(const_loaded, MOVE)
            for r in range(2):
                to = slice(CB * r, CB * (r + 1))
                sp.dma_start(mean_a[:, 1, to], group_mean[0:P, P:C]).then_inc(const_loaded, MOVE)
                sp.dma_start(mean_b[:, 1, to], group_mean[P:C, P:C]).then_inc(const_loaded, MOVE)

            def load_x(j):
                sp.dma_start(x_sb[:, 0, :], x[j, 0:P, :]).then_inc(x_loaded, MOVE)
                for r in range(2):
                    sp.dma_start(x_sb[CB * r:CB * (r + 1), 1, :], x[j, P:C, :]).then_inc(x_loaded, MOVE)

            load_x(0)

            def stack_pair(par, p):
                for h in (2 * p, 2 * p + 1):
                    for stack, row, parts in ((q_stack, D * h, (qk_hi, qk_lo, qk_hi)),
                                              (k_stack, C + D * h, (qk_hi, qk_hi, qk_lo))):
                        for n, part in enumerate(parts):
                            sp.dma_start(stack[D * n:D * (n + 1), par, h, :],
                                         part[row % P:row % P + D, row // P, :]).then_inc(stacked[p], MOVE)

            def step(st):
                b = st.b
                for s in range(SLOTS):
                    if s == 0 and st.maxima and not (isinstance(b, int) and b < -1):
                        if st.tail:
                            sp.wait_ge(scores_ready, SCORE_UNITS * SLOTS * b)
                        stack_pair(1 - st.parity, PAIRS - 1)
                    if s in SHIFT_SLOTS:
                        p = SHIFT_SLOTS[s]
                        last = p == PAIRS - 1
                        if st.shift_last if last else st.maxima:
                            j, par = (b, st.parity) if last else (b + 1, 1 - st.parity)
                            sp.wait_ge(shift_step, 2 * (PAIRS * j + p + 1))
                            for part in range(2):
                                sp.dma_start(
                                    q_stack[STACK + part:STACK + part + 1, par, 2 * p:2 * p + 2, :],
                                    shift_rows[:, part, :]).then_inc(shift_moved, MOVE)
                    if s == 4 and st.tail:
                        sp.dma_start(x_res[:, :, :],
                                     x[b - 1, :, :].rearrange("(t p) n -> p t n", p=OM)).then_inc(res_loaded, MOVE)
                    if s in NORM_SLOTS:
                        p = NORM_SLOTS[s]
                        last = p == PAIRS - 1
                        if st.tail if last else st.attend:
                            j = b - 1 if last else b
                            sp.wait_ge(norm_done, PAIRS * j + p + 1)
                            if p == 0 and st.tail:
                                sp.wait_ge(misc_filled, st.ordinal("proj", 3) + 1)
                            row = 2 * D * p
                            for half in range(HALVES):
                                sp.dma_start(
                                    attn[row % P:row % P + 2 * D, row // P, HALF * half:HALF * (half + 1)],
                                    heads_out[2 * D * half:2 * D * (half + 1), :]).then_inc(attn_moved, MOVE)
                    if s == LOAD_SLOT and st.project_in and not (isinstance(b, int) and b + 3 >= BATCH):
                        sp.wait_ge(xhat_ready, XHAT * (b + 3))
                        load_x(b + 3)
                    if s == PROJ_SLOTS[-1] + 1 and st.tail:
                        sp.wait_ge(misc_freed, st.ordinal("proj", 3) + 1)
                        sp.dma_start(out[b - 1, :, :].rearrange("(t p) n -> p t n", p=OM),
                                     y[:, :, :]).then_inc(y_stored, MOVE)
                    if st.project_in and s in (QK_SLOTS[3] + 1, QK_SLOTS[5] + 1):
                        p = 0 if s == QK_SLOTS[3] + 1 else 1
                        sp.wait_ge(misc_freed, st.ordinal("qk", 3 if p == 0 else 5) + 1)
                        if st.attend:
                            sp.wait_ge(scores_ready, SCORE_UNITS * (SLOTS * b + TILES * (p + 1)))
                        stack_pair(st.parity, p)

            run_steps(sp, step)
            sp.wait_ge(y_stored, MOVE * BATCH)

        @block.tensor
        def _(pe):
            pe.wait_ge(const_loaded, MOVE * 13)
            pe.wait_ge(setup, 3)
            for i in range(3):
                sec = slice(C * i, C * (i + 1))
                pe.matmul(scores_ps[:, i, 0:C], ones[:, :], xhat[:, 0, sec], start=True, stop=False)
                last = pe.matmul(scores_ps[:, i, 0:C], ones[0:CB, :], xhat[0:CB, 1, sec], start=False, stop=True)
            last.then_inc(l1_ready, 1)

            def fill(st, use):
                g, bank, kind, i = use
                ps = misc_ps[:, bank, :]
                if due(g - 1):
                    pe.wait_ge(misc_freed, g - 1)
                if kind == "max":
                    s, (a, half) = i[0], divmod(i[1], 2)
                    p, tile = divmod(s, TILES)
                    par, h = 1 - st.parity, 2 * p + a
                    if tile == 0 and i[1] == 0:
                        pe.wait_ge(stacked[p], MOVE * STACK_MOVES * (st.b + 2))
                    last = pe.matmul(ps, q_stack[0:STACK, par, h, P * tile:P * (tile + 1)],
                                     k_stack[0:STACK, par, h, HALF * half:HALF * (half + 1)],
                                     start=True, stop=True)
                elif kind == "shift":
                    j = st.b if i == PAIRS - 1 else st.b + 1
                    pe.wait_ge(neg_max_ready, PAIRS * j + i + 1)
                    last = pe.transpose(misc_ps[0:2 * TILES, bank, 0:P], neg_max[:, :], ident[:, :])
                elif kind in ("mean", "var"):
                    pe.wait_ge(stats_step, STATS * (st.b + 2) + (6 if kind == "mean" else 9))
                    for t in range(2):
                        per_chan = (chan_stats[:, 0, 0:1], chan_stats[0:CB, 1, 0:1]) if kind == "mean" else \
                            (chan_var[:, 0:1], chan_var[0:CB, 1:2])
                        pe.matmul(misc_ps[:, bank, t:t + 1], mean_a[:, t, :], per_chan[0], start=True, stop=False)
                        last = pe.matmul(misc_ps[:, bank, t:t + 1], mean_b[:, t, :], per_chan[1],
                                         start=False, stop=True)
                elif kind == "qk":
                    t, half = divmod(i, 2)
                    if i == 0:
                        pe.wait_ge(xlo_ready, 2 * (st.b + 3))
                    o, n, par = slice(P * t, P * (t + 1)), slice(HALF * half, HALF * (half + 1)), st.parity
                    pe.matmul(ps, w_hi[:, 0, o], xhat_a_hi[:, par, n], start=True, stop=False)
                    pe.matmul(ps, w_lo[:, 0, o], xhat_a_hi[:, par, n], start=False, stop=False)
                    pe.matmul(ps, w_hi[:, 0, o], xhat_a_lo[:, par, n], start=False, stop=False)
                    pe.matmul(ps, w_hi[:, 1, o], xhat_b[:, par, n], start=False, stop=False)
                    last = pe.matmul(ps, w_lo[0:CB, 1, o], xhat_b[0:CB, par, n], start=False, stop=True)
                elif kind == "v":
                    par, o = 1 - st.parity, slice(2 * C, 3 * C)
                    for t in range(2):
                        n = slice(P * (2 * i + t), P * (2 * i + t + 1))
                        to = misc_ps[:, bank, C * t:C * (t + 1)]
                        pe.matmul(to, xhat_a_hi[:, par, n], w_hi[:, 0, o], start=True, stop=False)
                        pe.matmul(to, xhat_a_hi[:, par, n], w_lo[:, 0, o], start=False, stop=False)
                        pe.matmul(to, xhat_a_lo[:, par, n], w_hi[:, 0, o], start=False, stop=False)
                        pe.matmul(to, xhat_b[:, par, n], w_hi[:, 1, o], start=False, stop=False)
                        last = pe.matmul(to, xhat_b[0:CB, par, n], w_lo[0:CB, 1, o], start=False, stop=True)
                elif kind == "proj":
                    t, half = divmod(i, 2)
                    if i == 0:
                        pe.wait_ge(attn_moved, MOVE * HALVES * PAIRS * st.b)
                    o, n = slice(OM * t, OM * (t + 1)), slice(HALF * half, HALF * (half + 1))
                    pe.matmul(misc_ps[0:OM, bank, :], wp[:, 0, o], attn[:, 0, n], start=True, stop=False)
                    last = pe.matmul(misc_ps[0:OM, bank, :], wp[0:CB, 1, o], attn[0:CB, 1, n],
                                     start=False, stop=True)
                last.then_inc(misc_filled, 1)

            def score(st, s, u):
                p, tile = divmod(s, TILES)
                a, half = divmod(u, 2)
                h, g = 2 * p + a, SCORE_UNITS * (SLOTS * st.b + s) + u
                if tile == 0 and u == 0:
                    pe.wait_ge(shift_moved, MOVE * 2 * (PAIRS * st.b + p + 1))
                if due(g - SCORE_BANKS + 1):
                    pe.wait_ge(probs_ready, g - SCORE_BANKS + 1)
                pe.matmul(scores_ps[:, u_bank(s, u), :],
                          k_stack[0:SHIFTED, st.parity, h, P * tile:P * (tile + 1)],
                          q_stack[0:SHIFTED, st.parity, h, HALF * half:HALF * (half + 1)],
                          start=True, stop=True).then_inc(scores_ready, 1)

            def weigh(b, par, s):
                p, tile = divmod(s, TILES)
                pe.wait_ge(probs_ready, SCORE_UNITS * (SLOTS * b + s + 1))
                if tile == 0 and due(PAIRS * b + p - 1):
                    pe.wait_ge(norm_done, PAIRS * b + p - 1)
                for half in range(HALVES):
                    for a in range(2):
                        at, h = D * (2 * half + a), 2 * p + a
                        last = pe.matmul(heads_ps[at:at + D, (par + p) % 2, :],
                                         v_sb[:, par, tile, D * h:D * (h + 1)],
                                         probs[:, a, s % RING, HALF * half:HALF * (half + 1)],
                                         start=(tile == 0), stop=(tile == TILES - 1))
                last.then_inc(heads_done, 1)

            def count(b, j):
                p, jj = divmod(j, TILES // 2)
                pe.wait_ge(pairs_added, 2 * (SLOTS // 2 * b + j + 1))
                if jj == 0 and due(PAIRS * b + p):
                    pe.wait_ge(norm_done, PAIRS * b + p)
                for half in range(HALVES):
                    for a in range(2):
                        at = D * (2 * half + a)
                        last = pe.matmul(sums_ps[at:at + D, :], ones_v[:, :],
                                         prob_pairs[:, a, j % 2, HALF * half:HALF * (half + 1)],
                                         start=(jj == 0), stop=(jj == TILES // 2 - 1))
                last.then_inc(sums_done, 1)

            pe.wait_ge(setup, SETUP)

            def step(st):
                for s in range(SLOTS):
                    uses = [(g, bank, kind, (s, i) if kind == "max" else i) for g, bank, kind, i in st.at_slot(s)]
                    units = [u for u in uses if u[2] == "max"]
                    others = [u for u in uses if u[2] != "max"]
                    for u in range(SCORE_UNITS):
                        if st.attend:
                            score(st, s, u)
                        if units:
                            fill(st, units[u])
                        if u == 1:
                            if s == 0 and st.tail:
                                weigh(st.b - 1, 1 - st.parity, SLOTS - 1)
                            elif s > 0 and st.attend:
                                weigh(st.b, st.parity, s - 1)
                    if s in (0, 2) and st.tail:
                        count(st.b - 1, SLOTS // 2 - 2 + s // 2)
                    elif s >= 4 and s % 2 == 0 and st.attend:
                        count(st.b, s // 2 - 2)
                    for use in others:
                        fill(st, use)

            run_steps(pe, step)

        @block.scalar
        def _(act):
            def step(st):
                for s in range(SLOTS):
                    if st.attend:
                        for u in range(SCORE_UNITS):
                            a, half = divmod(u, 2)
                            g = SCORE_UNITS * (SLOTS * st.b + s) + u
                            if u == 0 and due(SLOTS * st.b + s - RING + 1):
                                act.wait_ge(heads_done, SLOTS * st.b + s - RING + 1)
                                act.wait_ge(pairs_added, 2 * (SLOTS // 2 * st.b + (s - RING) // 2 + 1))
                            act.wait_ge(scores_ready, g + 1)
                            nc.scalar.activation(probs[:, a, s % RING, HALF * half:HALF * (half + 1)],
                                                 scores_ps[:, u_bank(s, u), :], ACT.Exp,
                                                 scale=exp_scale[:, 0:1]).then_inc(probs_ready, 1)
                    if st.project_in and s in XHAT_SLOTS:
                        k = XHAT_SLOTS.index(s)
                        t, hi = divmod(k, 2)
                        if k == 0:
                            act.wait_ge(rstd_step, 2 * (st.b + 3))
                            if due(2 * (st.b + 2)):
                                act.wait_ge(xlo_ready, 2 * (st.b + 2))
                        to = (xhat[:, t, :], (xhat_a_hi, xhat_b)[t][:, st.parity, :])[hi]
                        nc.scalar.activation(to, x_sb[:, t, :], ACT.Identity, bias=neg_mu_rstd[:, t:t + 1],
                                             scale=rstd[:, t:t + 1]).then_inc(xhat_ready, 1)
                    for g, bank, kind, i in st.at_slot(s):
                        if kind == "qk":
                            t, half = divmod(i, 2)
                            if i == 0 and due(st.b + 2):
                                for p in range(PAIRS):
                                    act.wait_ge(stacked[p], MOVE * STACK_MOVES * (st.b + 2))
                            act.wait_ge(misc_filled, g + 1)
                            nc.scalar.copy(qk_hi[:, t, HALF * half:HALF * (half + 1)],
                                           misc_ps[:, bank, :]).then_inc(qk_hi_ready, 1)

            run_steps(act, step)

        @block.gpsimd
        def _(pool):
            def step(st):
                for s in range(SLOTS):
                    if st.project_in and s == VAR_SLOT:
                        pool.wait_ge(misc_freed, st.ordinal("var", 0) + 1)
                        nc.gpsimd.tensor_tensor(rstd[:, :], var_eps[:, :], minus_half[:, :],
                                                ALU.pow).then_inc(rstd_step, 1)
                        pool.wait_ge(rstd_step, 2 * (st.b + 2) + 1)
                        nc.gpsimd.tensor_tensor(neg_mu_rstd[:, :], neg_mu[:, :], rstd[:, :],
                                                ALU.mult).then_inc(rstd_step, 1)
                    if st.project_in and s == XHAT_SLOTS[-1]:
                        pool.wait_ge(xhat_ready, XHAT * (st.b + 3))
                        nc.gpsimd.tensor_tensor(xhat_a_lo[:, st.parity, :], xhat[:, 0, :],
                                                xhat_a_hi[:, st.parity, :], ALU.subtract).then_inc(xlo_ready, 1)
                        pool.wait_ge(xlo_ready, 2 * (st.b + 2) + 1)
                        nc.gpsimd.tensor_tensor(xhat_b[CB:P, st.parity, :], xhat[CB:P, 1, :],
                                                xhat_b[CB:P, st.parity, :], ALU.subtract).then_inc(xlo_ready, 1)
                        pool.wait_ge(xlo_ready, 2 * (st.b + 3))
                    if st.attend and s % 2 == 1:
                        j = s // 2
                        for a in range(2):
                            pool.wait_ge(probs_ready, SCORE_UNITS * (SLOTS * st.b + s) + 2 * (a + 1))
                            if a == 0 and due(SLOTS // 2 * st.b + j - 1):
                                pool.wait_ge(sums_done, SLOTS // 2 * st.b + j - 1)
                            nc.gpsimd.tensor_tensor(prob_pairs[:, a, j % 2, :], probs[:, a, (s - 1) % RING, :],
                                                    probs[:, a, s % RING, :], ALU.add).then_inc(pairs_added, 1)

            run_steps(pool, step)

        @block.vector
        def _(dve):
            nc.vector.memset(minus_half[:, :], -0.5)
            nc.vector.memset(k_stack[STACK:SHIFTED, :, :, :], SHIFT)
            nc.vector.memset(ones[:, :], 1.0).then_inc(setup, 1)
            dve.wait_ge(const_loaded, MOVE * 13)
            for t in range(2):
                nc.vector.scalar_tensor_tensor(out=xhat[:, t, 0:3 * C], in0=w_f32[:, t, :], scalar=-1.0,
                                               in1=w_f32[:, t, :], op0=ALU.mult,
                                               op1=ALU.max).then_inc(setup, 1)
            dve.wait_ge(l1_ready, 1)
            nc.vector.tensor_reduce(l1_max[:, :], scores_ps[:, :, 0:C], AX_X, ALU.max).then_inc(setup, 1)
            dve.wait_ge(setup, 4)
            nc.vector.tensor_scalar(unscale[:, :], l1_max[:, :], XHAT_MAX / LIMIT, 1e-30,
                                    ALU.mult, ALU.max).then_inc(setup, 1)
            dve.wait_ge(setup, 5)
            nc.vector.reciprocal(rescale[:, :], unscale[:, :]).then_inc(setup, 1)
            nc.vector.tensor_scalar(exp_scale[:, :], unscale[:, 0:1], unscale[:, 1:2], SCALE,
                                    ALU.mult, ALU.mult).then_inc(setup, 1)
            dve.wait_ge(setup, 7)
            nc.vector.tensor_scalar(ones_v[:, :], ones[:, 0:D], rescale[:, 2:3], None,
                                    ALU.mult).then_inc(setup, 1)
            for t in range(2):
                for i in range(3):
                    sec = slice(C * i, C * (i + 1))
                    nc.vector.tensor_scalar(w_f32[:, t, sec], w_f32[:, t, sec], rescale[:, i:i + 1], None,
                                            ALU.mult).then_inc(setup, 1)
            dve.wait_ge(setup, 14)
            nc.vector.tensor_copy(w_hi[:, :, :], w_f32[:, :, :]).then_inc(setup, 1)
            dve.wait_ge(setup, 15)
            nc.vector.tensor_tensor(w_lo[:, :, :], w_f32[:, :, :], w_hi[:, :, :], ALU.subtract).then_inc(setup, 1)

            def statistics(st):
                j = st.b + 2
                dve.wait_ge(x_loaded, MOVE * 3 * (j + 1))
                for t in range(2):
                    for half in range(HALVES):
                        nc.vector.bn_stats(half_stats[:, t, half, :],
                                           x_sb[:, t, HALF * half:HALF * (half + 1)]).then_inc(stats_step, 1)
                dve.wait_ge(stats_step, STATS * j + 4)
                dve.sem_inc(halves_seen, 1)
                for t in range(2):
                    nc.vector.bn_aggr(chan_stats[:, t, :],
                                      half_stats[:, t, :, :].rearrange("p a b -> p (a b)")).then_inc(stats_step, 1)

            def read(st, s, use):
                g, bank, kind, i = use
                dve.wait_ge(misc_filled, g + 1)
                if kind == "max":
                    a, half = divmod(i, 2)
                    tile = s % TILES
                    if tile == 0 and i == 0 and due(PAIRS * (st.b + 1) + s // TILES):
                        dve.wait_ge(neg_max_ready, PAIRS * (st.b + 1) + s // TILES)
                    nc.vector.tensor_reduce(half_max[:, a, tile, half:half + 1], misc_ps[:, bank, :], AX_X,
                                            ALU.max).then_inc(misc_freed, 1)
                elif kind == "shift":
                    j = st.b if i == PAIRS - 1 else st.b + 1
                    k = PAIRS * j + i
                    if due(k):
                        dve.wait_ge(shift_moved, MOVE * 2 * k)
                    turned = misc_ps[0:2 * TILES, bank, 0:P]
                    nc.vector.tensor_scalar(shift_rows[:, 0, :], turned, 1.0 / SHIFT, None,
                                            ALU.mult).then_inc(shift_step, 1)
                    dve.wait_ge(shift_step, 2 * k + 1)
                    nc.vector.scalar_tensor_tensor(out=shift_rows[:, 1, :], in0=turned, scalar=1.0 / SHIFT,
                                                   in1=shift_rows[:, 0, :], op0=ALU.mult,
                                                   op1=ALU.subtract).then_inc(shift_step, 1)
                    dve.wait_ge(shift_step, 2 * k + 2)
                    dve.sem_inc(misc_freed, 1)
                elif kind == "mean":
                    j = st.b + 2
                    nc.vector.tensor_scalar(neg_mu[:, :], misc_ps[:, bank, 0:2], -1.0, None,
                                            ALU.mult).then_inc(misc_freed, 1)
                    dve.wait_ge(misc_freed, g + 1)
                    nc.vector.tensor_tensor(mu_off[:, :], chan_stats[:, :, 0], neg_mu[:, :],
                                            ALU.add).then_inc(stats_step, 1)
                    dve.wait_ge(stats_step, STATS * j + 7)
                    nc.vector.tensor_tensor(mu_off2[:, :], mu_off[:, :], mu_off[:, :],
                                            ALU.mult).then_inc(stats_step, 1)
                    dve.wait_ge(stats_step, STATS * j + 8)
                    nc.vector.tensor_tensor(chan_var[:, :], chan_stats[:, :, 1], mu_off2[:, :],
                                            ALU.add).then_inc(stats_step, 1)
                elif kind == "var":
                    nc.vector.tensor_scalar(var_eps[:, :], misc_ps[:, bank, 0:2], EPS, None,
                                            ALU.add).then_inc(misc_freed, 1)
                elif kind == "qk":
                    t, half = divmod(i, 2)
                    n = slice(HALF * half, HALF * (half + 1))
                    dve.wait_ge(qk_hi_ready, 6 * (st.b + 2) + i + 1)
                    nc.vector.tensor_tensor(qk_lo[:, t, n], misc_ps[:, bank, :], qk_hi[:, t, n],
                                            ALU.subtract).then_inc(misc_freed, 1)
                elif kind == "v":
                    nc.vector.tensor_copy(v_sb[:, 1 - st.parity, 2 * i:2 * i + 2, :].rearrange("p t c -> p (t c)"),
                                          misc_ps[:, bank, 0:2 * C]).then_inc(misc_freed, 1)
                elif kind == "proj":
                    t, half = divmod(i, 2)
                    n = slice(HALF * half, HALF * (half + 1))
                    if i == 0:
                        dve.wait_ge(res_loaded, MOVE * st.b)
                        if due(st.b - 1):
                            dve.wait_ge(y_stored, MOVE * (st.b - 1))
                    nc.vector.scalar_tensor_tensor(out=y[:, t, n], in0=misc_ps[0:OM, bank, :],
                                                   scalar=bias[:, t:t + 1], in1=x_res[:, t, n], op0=ALU.add,
                                                   op1=ALU.add).then_inc(misc_freed, 1)

            def normalise(b, par, p):
                k = PAIRS * b + p
                dve.wait_ge(sums_done, TILES // 2 * (k + 1))
                if due(k):
                    dve.wait_ge(norm_done, k)
                nc.vector.reciprocal(sums_inv[:, :], sums_ps[:, :]).then_inc(inverted, 1)
                dve.wait_ge(inverted, k + 1)
                if due(k):
                    dve.wait_ge(attn_moved, MOVE * HALVES * k)
                nc.vector.tensor_tensor(heads_out[:, :], heads_ps[:, (par + p) % 2, :], sums_inv[:, :],
                                        ALU.mult).then_inc(norm_done, 1)

            def step(st):
                for s in range(SLOTS):
                    if s == 0 and st.project_in:
                        statistics(st)
                    if s in NORM_SLOTS:
                        p = NORM_SLOTS[s]
                        if p == PAIRS - 1:
                            if st.tail:
                                normalise(st.b - 1, 1 - st.parity, p)
                        elif st.attend:
                            normalise(st.b, st.parity, p)
                    uses = st.at_slot(s)
                    for use in uses:
                        read(st, s, use)
                    if s % TILES == TILES - 1 and st.maxima:
                        last = [g for g, _, kind, _ in uses if kind == "max"][-1]
                        dve.wait_ge(misc_freed, last + 1)
                        nc.vector.tensor_reduce(neg_max[:, :],
                                                half_max[:, :, :, :].rearrange("p a t h -> p (a t) h"),
                                                AX_X, ALU.max, negate=True).then_inc(neg_max_ready, 1)

            run_steps(dve, step)


SETUP = 16


def u_bank(s, u):
    return (SCORE_UNITS * s + u) % SCORE_BANKS


def kernel(x, L0_conv_qkv_w, L0_conv_proj_w, L0_conv_proj_b):
    import concourse.bacc as bacc
    from concourse.bass_utils import run_bass_kernel_spmd

    channel = np.arange(C) // GROUP
    arrays = {
        "x": np.ascontiguousarray(x).reshape(BATCH, C, N),
        "qkv_wT": np.ascontiguousarray(np.asarray(L0_conv_qkv_w).T),
        "proj_wT": np.ascontiguousarray(np.asarray(L0_conv_proj_w).T),
        "proj_b": np.ascontiguousarray(np.asarray(L0_conv_proj_b).reshape(2, OM).T),
        "group_mean": np.where(channel[:, None] == channel[None, :], np.float32(1.0 / GROUP), np.float32(0.0)),
        "identity": np.eye(P, dtype=np.float32),
    }
    nc = bacc.Bacc("TRN2", target_bir_lowering=False, num_devices=1)
    ins = [nc.dram_tensor(name, a.shape, mybir.dt.from_np(a.dtype), kind="ExternalInput").ap()
           for name, a in arrays.items()]
    out = nc.dram_tensor("out", (BATCH, C, N), F32, kind="ExternalOutput").ap()
    group_norm_attention(nc, *ins, out)
    r = run_bass_kernel_spmd(nc, [arrays], core_ids=[0])
    return r.results[0]["out"].reshape(BATCH, C, H, W)
```

```python
from contextlib import ExitStack
from math import sqrt

import numpy as np

import concourse.bass as bass
from concourse import mybir

F32 = mybir.dt.float32
F16 = mybir.dt.float16
ALU = mybir.AluOpType
ACT = mybir.ActivationFunctionType
AX_X = mybir.AxisListType.X

BATCH = 16
C = 192
H = W = 32
N = H * W
HEADS = 6
D = C // HEADS
GROUPS = 32
GROUP = C // GROUPS
EPS = 1e-5
SCALE = D ** -0.5

P = 128
HALF = 512
HALVES = N // HALF
TILES = N // P
PAIRS = HEADS // 2
SLOTS = PAIRS * TILES
CB = C - P
SCORE_UNITS = 4
SCORE_BANKS = 3
RING = 4
PAIR_RING = 4
OM = C // 2

STACK = 3 * D
SHIFTED = STACK + 2
SHIFT = 2.0 ** 15
LIMIT = 8192.0
XHAT_MAX = sqrt(GROUP * N)
PROJ_LIMIT = 64.0

SHIFT_SLOTS = {1: 2, 9: 0, 17: 1}
MEAN_SLOT, VAR_SLOT = 2, 3
XHAT_SLOTS = (4, 5, 6, 7)
V_SLOTS = (4, 5, 6, 7)
QK_SLOTS = (10, 11, 12, 13, 14, 15)
PROJ_SLOTS = (16, 18, 19, 20)
STACK_SLOTS = {14: 0, 17: 1}
LOAD_SLOT = 8
HEADS_TAKEN = TILES
SUMS_TAKEN = TILES + 4
SUMS_TURNED = TILES + 5
DIVIDED = TILES + 9
MOVED = (22, 19, 19)
QUAD = 4
QUAD_ADDED = QUAD + 2
QUAD_COUNTED = QUAD + 4

STATS = 9
XHAT = 4
LO = 2
MOVE = 16
ATTN_MOVES = 4
STACK_MOVES = 12


class Step:

    def __init__(self, b, at, extras):
        self.b = b
        self.parity = at % 2
        self.attend = 0 <= at < BATCH
        self.maxima = 0 <= at + 1 < BATCH
        self.project_in = 0 <= at + 2 < BATCH
        self.tail = 0 <= at - 1 < BATCH
        self.extras = extras

    def extra(self, s):
        if s in SHIFT_SLOTS and (self.attend if SHIFT_SLOTS[s] == PAIRS - 1 else self.maxima):
            return "shift", SHIFT_SLOTS[s]
        if self.project_in and s in (MEAN_SLOT, VAR_SLOT):
            return ("mean", 0) if s == MEAN_SLOT else ("var", 0)
        if self.maxima and s in V_SLOTS:
            return "v", V_SLOTS.index(s)
        if self.project_in and s in QK_SLOTS:
            return "qk", QK_SLOTS.index(s)
        if self.tail and s in PROJ_SLOTS:
            return "proj", PROJ_SLOTS.index(s)
        return None

    def ordinal(self, slot):
        return self.extras + sum(self.extra(s) is not None for s in range(slot))

    def due(self, s, offset, every):
        at = s - offset
        if at % every == 0 and at >= 0 and self.attend:
            return [(self.b, self.parity, at // every)]
        if at % every == 0 and -SLOTS <= at < 0 and self.tail:
            return [(self.b - 1, 1 - self.parity, (at + SLOTS) // every)]
        return []

    def moved(self, s):
        return [x for p in range(PAIRS) for x in self.due(s, MOVED[p], TILES) if x[2] == p]


SPREAD = 4 * HALF // P
SETUP = 18

LOOP_FIRST, LOOP_END = 1, 13


def run_steps(eng, step):
    extras = 0
    for at in range(-2, LOOP_FIRST):
        st = Step(at, at, extras)
        step(st)
        extras = st.ordinal(SLOTS)
    per = Step(LOOP_FIRST, LOOP_FIRST, 0).ordinal(SLOTS)
    with eng.Fori(0, (LOOP_END - LOOP_FIRST) // 2) as i:
        for k in range(2):
            step(Step(2 * i + (LOOP_FIRST + k), LOOP_FIRST + k, 2 * per * i + (extras + per * k)))
    extras += per * (LOOP_END - LOOP_FIRST)
    for at in range(LOOP_END, BATCH + 1):
        st = Step(at, at, extras)
        step(st)
        extras = st.ordinal(SLOTS)


def due(count):
    return not isinstance(count, int) or count > 0


def group_norm_attention(nc, x, qkv_wT, proj_wT, proj_b, group_mean, identity, out):
    with ExitStack() as ctx:
        def sb(name, shape, dt):
            return ctx.enter_context(nc.sbuf_tensor(name, shape, dt))

        def psum(name, shape):
            return ctx.enter_context(nc.psum_tensor(name, shape, F32))

        def sem(name):
            return ctx.enter_context(nc.semaphore(name))

        scores_ps = psum("scores_ps", [P, SCORE_BANKS, HALF])
        max_ps = psum("max_ps", [P, 2, HALF])
        extra_ps = psum("extra_ps", [P, HALF])
        heads_ps = psum("heads_ps", [P, HALF])
        sums_ps = psum("sums_ps", [P, HALF])

        q_stack = sb("q_stack", [P, 2, HEADS, N], F16)
        k_stack = sb("k_stack", [P, 2, HEADS, N], F16)
        v_sb = sb("v_sb", [P, 2, TILES, C], F32)
        probs = sb("probs", [P, 2, RING, N], F32)
        prob_pairs = sb("prob_pairs", [P, 2, PAIR_RING, N], F32)
        xhat_a_hi = sb("xhat_a_hi", [P, 2, N], F16)
        xhat_a_lo = sb("xhat_a_lo", [P, 2, N], F16)
        xhat_b = sb("xhat_b", [P, 2, N], F16)
        xhat = sb("xhat", [P, 2, N], F32)
        x_sb = sb("x_sb", [P, 2, N], F32)
        qk_hi = sb("qk_hi", [P, 3, N], F16)
        qk_lo = sb("qk_lo", [P, 3, N], F16)
        heads_sb = sb("heads_sb", [P, 2, HALF], F32)
        sums_sb = sb("sums_sb", [P, HALF], F32)
        sums_spread = sb("sums_spread", [P, SPREAD], F32)
        inv_spread = sb("inv_spread", [P, SPREAD], F32)
        inv_rows = nc.dram_tensor("inv_rows", (4, HALF), F32, kind="Internal").ap()
        inv_sb = sb("inv_sb", [P, HALF], F32)
        heads_out = sb("heads_out", [P, HALF], F32)
        heads_hi = sb("heads_hi", [P, HALF], F16)
        heads_lo = sb("heads_lo", [P, HALF], F16)
        attn_a_hi = sb("attn_a_hi", [P, N], F16)
        attn_a_lo = sb("attn_a_lo", [P, N], F16)
        attn_b = sb("attn_b", [P, N], F16)
        x_res = sb("x_res", [OM, 2, N], F32)
        projected = sb("projected", [OM, 2, HALF], F32)

        w_f32 = prob_pairs[:, 0, 0:2, 0:3 * C]
        wp_f32 = prob_pairs[:, 0, 2:4, 0:C]
        w_abs = prob_pairs[:, 1, 0:2, 0:3 * C]
        wp_abs = prob_pairs[:, 1, 2:4, 0:C]
        w_hi = sb("w_hi", [P, 2, 3 * C], F16)
        w_lo = sb("w_lo", [P, 2, 3 * C], F16)
        wp_hi = sb("wp_hi", [P, 2, C], F16)
        wp_lo = sb("wp_lo", [P, 2, C], F16)
        bias = sb("bias", [OM, 2], F32)
        mean_a = sb("mean_a", [P, 2, P], F32)
        mean_b = sb("mean_b", [CB, 2, P], F32)
        ident = sb("ident", [P, P], F32)
        ones = sb("ones", [P, P], F32)
        l1_max = sb("l1_max", [P, 4], F32)
        unscale = sb("unscale", [P, 4], F32)
        rescale = sb("rescale", [P, 4], F32)
        proj_unscale = sb("proj_unscale", [P, 1], F32)
        exp_scale = sb("exp_scale", [P, 1], F32)

        half_stats = sb("half_stats", [P, 2, HALVES, 6], F32)
        chan_stats = sb("chan_stats", [P, 2, 2], F32)
        neg_mu = sb("neg_mu", [P, 2], F32)
        mu_off = sb("mu_off", [P, 2], F32)
        mu_off2 = sb("mu_off2", [P, 2], F32)
        chan_var = sb("chan_var", [P, 2], F32)
        var_eps = sb("var_eps", [P, 2], F32)
        minus_half = sb("minus_half", [P, 2], F32)
        rstd = sb("rstd", [P, 2], F32)
        neg_mu_rstd = sb("neg_mu_rstd", [P, 2], F32)
        half_max = sb("half_max", [P, 2, TILES, HALVES], F32)
        neg_max = sb("neg_max", [P, 2 * TILES], F32)
        shift_rows = sb("shift_rows", [2 * TILES, 2, P], F16)

        const_loaded = sem("const_loaded")
        setup = sem("setup")
        l1_ready = sem("l1_ready")
        x_loaded = sem("x_loaded")
        stats_step = sem("stats_step")
        halves_seen = sem("halves_seen")
        rstd_step = sem("rstd_step")
        xhat_ready = sem("xhat_ready")
        xlo_ready = sem("xlo_ready")
        max_filled = [sem(f"max_filled{i}") for i in range(2)]
        max_read = [sem(f"max_read{i}") for i in range(2)]
        extra_filled = sem("extra_filled")
        extra_freed = sem("extra_freed")
        qk_hi_ready = sem("qk_hi_ready")
        stacked = [sem(f"stacked{p}") for p in range(PAIRS)]
        neg_max_ready = sem("neg_max_ready")
        shift_step = sem("shift_step")
        shift_moved = sem("shift_moved")
        scores_ready = sem("scores_ready")
        probs_ready = sem("probs_ready")
        pairs_added = sem("pairs_added")
        heads_done = sem("heads_done")
        sums_done = sem("sums_done")
        quads_added = sem("quads_added")
        heads_taken = sem("heads_taken")
        sums_taken = sem("sums_taken")
        sums_spread_out = sem("sums_spread_out")
        inverted = sem("inverted")
        inv_gathered = sem("inv_gathered")
        inv_broadcast = sem("inv_broadcast")
        divided = sem("divided")
        heads_hi_ready = sem("heads_hi_ready")
        heads_lo_ready = sem("heads_lo_ready")
        proj_taken = sem("proj_taken")
        residual_added = sem("residual_added")
        attn_moved = sem("attn_moved")
        res_loaded = sem("res_loaded")
        y_stored = sem("y_stored")

        block = ctx.enter_context(nc.Block())

        @block.sync
        def _(sp):
            sp.dma_start(w_f32[:, 0, :], qkv_wT[0:P, :]).then_inc(const_loaded, MOVE)
            for r in range(2):
                sp.dma_start(w_f32[CB * r:CB * (r + 1), 1, :], qkv_wT[P:C, :]).then_inc(const_loaded, MOVE)
            sp.dma_start(wp_f32[:, 0, :], proj_wT[0:P, :]).then_inc(const_loaded, MOVE)
            for r in range(2):
                sp.dma_start(wp_f32[CB * r:CB * (r + 1), 1, :], proj_wT[P:C, :]).then_inc(const_loaded, MOVE)
            sp.dma_start(bias[:, :], proj_b).then_inc(const_loaded, MOVE)
            sp.dma_start(ident[:, :], identity).then_inc(const_loaded, MOVE)
            sp.dma_start(mean_a[:, 0, :], group_mean[0:P, 0:P]).then_inc(const_loaded, MOVE)
            sp.dma_start(mean_b[:, 0, :], group_mean[P:C, 0:P]).then_inc(const_loaded, MOVE)
            for r in range(2):
                to = slice(CB * r, CB * (r + 1))
                sp.dma_start(mean_a[:, 1, to], group_mean[0:P, P:C]).then_inc(const_loaded, MOVE)
                sp.dma_start(mean_b[:, 1, to], group_mean[P:C, P:C]).then_inc(const_loaded, MOVE)

            def load_x(j):
                sp.dma_start(x_sb[:, 0, :], x[j, 0:P, :]).then_inc(x_loaded, MOVE)
                for r in range(2):
                    sp.dma_start(x_sb[CB * r:CB * (r + 1), 1, :], x[j, P:C, :]).then_inc(x_loaded, MOVE)

            load_x(0)
            sp.sem_inc(y_stored, MOVE)

            def stack_pair(par, p):
                for h in (2 * p, 2 * p + 1):
                    for stack, row, parts in ((q_stack, D * h, (qk_hi, qk_lo, qk_hi)),
                                              (k_stack, C + D * h, (qk_hi, qk_hi, qk_lo))):
                        for n, part in enumerate(parts):
                            sp.dma_start(stack[D * n:D * (n + 1), par, h, :],
                                         part[row % P:row % P + D, row // P, :]).then_inc(stacked[p], MOVE)

            def step(st):
                b = st.b
                for s in range(SLOTS):
                    if s == 0 and st.maxima:
                        if st.tail:
                            sp.wait_ge(scores_ready, SCORE_UNITS * SLOTS * b)
                        stack_pair(1 - st.parity, PAIRS - 1)
                    if s > 0 and st.extra(s - 1) is not None and st.extra(s - 1)[0] == "shift":
                        p = st.extra(s - 1)[1]
                        j, par = (b, st.parity) if p == PAIRS - 1 else (b + 1, 1 - st.parity)
                        sp.wait_ge(shift_step, 2 * (PAIRS * j + p + 1))
                        for part in range(2):
                            sp.dma_start(q_stack[STACK + part:STACK + part + 1, par, 2 * p:2 * p + 2, :],
                                         shift_rows[:, part, :]).then_inc(shift_moved, MOVE)
                    for j, par, p in st.due(s, SUMS_TURNED, TILES):
                        k = PAIRS * j + p
                        sp.wait_ge(sums_taken, k + 1)
                        sp.dma_start(sums_spread[:, :], sums_sb[0:P:D, :]
                                     ).then_inc(sums_spread_out, MOVE)
                    for j, par, p in st.due(s, SUMS_TURNED + 1, TILES):
                        k = PAIRS * j + p
                        sp.wait_ge(inverted, k + 1)
                        sp.dma_start(inv_rows[:, :].rearrange("g (q n) -> (g q) n", n=SPREAD),
                                     inv_spread[:, :]).then_inc(inv_gathered, MOVE)
                        sp.wait_ge(inv_gathered, MOVE * (k + 1))
                        if due(k):
                            sp.wait_ge(divided, k)
                        for g in range(4):
                            sp.dma_start(inv_sb[D * g:D * (g + 1), :],
                                         inv_rows[g, :].partition_broadcast(D)).then_inc(inv_broadcast, MOVE)
                    for j, par, p in st.moved(s):
                        if p == 0 and st.tail:
                            sp.wait_ge(residual_added, 4 * b)
                        else:
                            sp.wait_ge(heads_lo_ready, PAIRS * j + p + 1)
                        for half in range(HALVES):
                            n, rows = slice(HALF * half, HALF * (half + 1)), slice(2 * D * half, 2 * D * (half + 1))
                            for lo, (to, row) in enumerate((((attn_a_hi, 0), (attn_a_lo, 0)),
                                                            ((attn_a_hi, 2 * D), (attn_a_lo, 2 * D)),
                                                            ((attn_b, 0), (attn_b, 2 * D)))[p]):
                                sp.dma_start(to[row:row + 2 * D, n],
                                             (heads_hi, heads_lo)[lo][rows, :]).then_inc(attn_moved, MOVE)
                    if s == 4 and st.tail:
                        sp.wait_ge(y_stored, MOVE * b)
                        sp.dma_start(x_res[:, :, :],
                                     x[b - 1, :, :].rearrange("(t p) n -> p t n", p=OM)).then_inc(res_loaded, MOVE)
                    if s == LOAD_SLOT and st.project_in and not (isinstance(b, int) and b + 3 >= BATCH):
                        sp.wait_ge(xhat_ready, XHAT * (b + 3))
                        load_x(b + 3)
                    if s in STACK_SLOTS and st.project_in:
                        p = STACK_SLOTS[s]
                        sp.wait_ge(extra_freed, st.ordinal(QK_SLOTS[3 if p == 0 else 5]) + 1)
                        if st.attend:
                            sp.wait_ge(scores_ready, SCORE_UNITS * (SLOTS * b + TILES * (p + 1)))
                        stack_pair(st.parity, p)
                    if s == SLOTS - 1 and st.tail:
                        sp.wait_ge(residual_added, 4 * b)
                        sp.dma_start(out[b - 1, :, :].rearrange("(t p) n -> p t n", p=OM),
                                     x_res[:, :, :]).then_inc(y_stored, MOVE)

            run_steps(sp, step)
            sp.wait_ge(y_stored, MOVE * (BATCH + 1))

        @block.tensor
        def _(pe):
            pe.wait_ge(setup, 5)
            for i in range(4):
                ps = extra_ps[:, 0:C] if i == 3 else scores_ps[:, i, 0:C]
                w = (wp_abs[:, :, :] if i == 3 else w_abs[:, :, C * i:C * (i + 1)])
                pe.matmul(ps, ones[:, :], w[:, 0, :], start=True, stop=False)
                last = pe.matmul(ps, ones[0:CB, :], w[0:CB, 1, :], start=False, stop=True)
            last.then_inc(l1_ready, 1)

            def row_max(st, s, u):
                p, tile = divmod(s, TILES)
                a, half = divmod(u, 2)
                par, h, g = 1 - st.parity, 2 * p + a, 2 * (SLOTS * (st.b + 1) + s) + a
                if tile == 0 and u == 0:
                    pe.wait_ge(stacked[p], MOVE * STACK_MOVES * (st.b + 2))
                if due(g):
                    pe.wait_ge(max_read[half], g)
                pe.matmul(max_ps[:, half, :], q_stack[0:STACK, par, h, P * tile:P * (tile + 1)],
                          k_stack[0:STACK, par, h, HALF * half:HALF * (half + 1)],
                          start=True, stop=True).then_inc(max_filled[half], 1)

            def fill(st, s):
                kind, i = st.extra(s)
                g = st.ordinal(s)
                if due(g):
                    pe.wait_ge(extra_freed, g)
                if kind == "shift":
                    j = st.b if i == PAIRS - 1 else st.b + 1
                    pe.wait_ge(neg_max_ready, PAIRS * j + i + 1)
                    last = pe.transpose(extra_ps[0:2 * TILES, 0:P], neg_max[:, :], ident[:, :])
                elif kind in ("mean", "var"):
                    pe.wait_ge(stats_step, STATS * (st.b + 2) + (6 if kind == "mean" else 9))
                    for t in range(2):
                        per_chan = (chan_stats[:, 0, 0:1], chan_stats[0:CB, 1, 0:1]) if kind == "mean" else \
                            (chan_var[:, 0:1], chan_var[0:CB, 1:2])
                        pe.matmul(extra_ps[:, t:t + 1], mean_a[:, t, :], per_chan[0], start=True, stop=False)
                        last = pe.matmul(extra_ps[:, t:t + 1], mean_b[:, t, :], per_chan[1],
                                         start=False, stop=True)
                elif kind == "qk":
                    t, half = divmod(i, 2)
                    if i == 0:
                        pe.wait_ge(xlo_ready, LO * (st.b + 3))
                    o, n, par = slice(P * t, P * (t + 1)), slice(HALF * half, HALF * (half + 1)), st.parity
                    last = product(extra_ps[:, :], w_hi[:, :, o], w_lo[:, :, o], xhat_a_hi[:, par, n],
                                   xhat_a_lo[:, par, n], xhat_b[:, par, n])
                elif kind == "v":
                    par, o = 1 - st.parity, slice(2 * C, 3 * C)
                    for t in range(2):
                        n = slice(P * (2 * i + t), P * (2 * i + t + 1))
                        to = extra_ps[:, C * t:C * (t + 1)]
                        pe.matmul(to, xhat_a_hi[:, par, n], w_hi[:, 0, o], start=True, stop=False)
                        pe.matmul(to, xhat_a_hi[:, par, n], w_lo[:, 0, o], start=False, stop=False)
                        pe.matmul(to, xhat_a_lo[:, par, n], w_hi[:, 0, o], start=False, stop=False)
                        pe.matmul(to, xhat_b[:, par, n], w_hi[:, 1, o], start=False, stop=False)
                        last = pe.matmul(to, xhat_b[0:CB, par, n], w_lo[0:CB, 1, o], start=False, stop=True)
                elif kind == "proj":
                    t, half = divmod(i, 2)
                    if i == 0:
                        pe.wait_ge(attn_moved, MOVE * ATTN_MOVES * PAIRS * st.b)
                    o, n = slice(OM * t, OM * (t + 1)), slice(HALF * half, HALF * (half + 1))
                    last = product(extra_ps[0:OM, :], wp_hi[:, :, o], wp_lo[:, :, o], attn_a_hi[:, n],
                                   attn_a_lo[:, n], attn_b[:, n])
                last.then_inc(extra_filled, 1)

            def product(to, hi, lo, a_hi, a_lo, b):
                pe.matmul(to, hi[:, 0, :], a_hi, start=True, stop=False)
                pe.matmul(to, lo[:, 0, :], a_hi, start=False, stop=False)
                pe.matmul(to, hi[:, 0, :], a_lo, start=False, stop=False)
                pe.matmul(to, hi[:, 1, :], b, start=False, stop=False)
                return pe.matmul(to, lo[0:CB, 1, :], b[0:CB, :], start=False, stop=True)

            def score(st, s, u):
                p, tile = divmod(s, TILES)
                a, half = divmod(u, 2)
                h, g = 2 * p + a, SCORE_UNITS * (SLOTS * st.b + s) + u
                if tile == 0 and u == 0:
                    pe.wait_ge(shift_moved, MOVE * 2 * (PAIRS * st.b + p + 1))
                if due(g - SCORE_BANKS + 1):
                    pe.wait_ge(probs_ready, g - SCORE_BANKS + 1)
                pe.matmul(scores_ps[:, u_bank(s, u), :],
                          k_stack[0:SHIFTED, st.parity, h, P * tile:P * (tile + 1)],
                          q_stack[0:SHIFTED, st.parity, h, HALF * half:HALF * (half + 1)],
                          start=True, stop=True).then_inc(scores_ready, 1)

            def weigh(b, par, s):
                p, tile = divmod(s, TILES)
                pe.wait_ge(probs_ready, SCORE_UNITS * (SLOTS * b + s + 1))
                if tile == 0 and due(PAIRS * b + p):
                    pe.wait_ge(heads_taken, PAIRS * b + p)
                for half in range(HALVES):
                    for a in range(2):
                        at, h = D * (2 * half + a), 2 * p + a
                        last = pe.matmul(heads_ps[at:at + D, :],
                                         v_sb[:, par, tile, D * h:D * (h + 1)],
                                         probs[:, a, s % RING, HALF * half:HALF * (half + 1)],
                                         start=(tile == 0), stop=(tile == TILES - 1))
                last.then_inc(heads_done, 1)

            def count(b, q):
                p, first = divmod(q, 2)
                pe.wait_ge(quads_added, 4 * (SLOTS // QUAD * b + q + 1))
                if first == 0 and due(PAIRS * b + p):
                    pe.wait_ge(sums_taken, PAIRS * b + p)
                for half in range(HALVES):
                    for a in range(2):
                        at = D * (2 * half + a)
                        last = pe.matmul(sums_ps[at:at + D, :], ones[:, 0:D],
                                         prob_pairs[:, a, (2 * q + 1) % PAIR_RING, HALF * half:HALF * (half + 1)],
                                         start=(first == 0), stop=(first == 1))
                last.then_inc(sums_done, 1)

            pe.wait_ge(setup, SETUP)

            def step(st):
                for s in range(SLOTS):
                    for u in range(SCORE_UNITS):
                        if st.attend:
                            score(st, s, u)
                        if u == 1:
                            if s == 0 and st.tail:
                                weigh(st.b - 1, 1 - st.parity, SLOTS - 1)
                            elif s > 0 and st.attend:
                                weigh(st.b, st.parity, s - 1)
                        if u == 3:
                            if st.extra(s) is not None:
                                fill(st, s)
                            for j, par, q in st.due(s, QUAD_COUNTED, QUAD):
                                count(j, q)
                        if st.maxima:
                            row_max(st, s, u)

            run_steps(pe, step)

        @block.scalar
        def _(act):
            def step(st):
                for s in range(SLOTS):
                    if st.attend:
                        for u in range(SCORE_UNITS):
                            a, half = divmod(u, 2)
                            g = SCORE_UNITS * (SLOTS * st.b + s) + u
                            if u == 0 and due(SLOTS * st.b + s - RING + 1):
                                act.wait_ge(heads_done, SLOTS * st.b + s - RING + 1)
                                act.wait_ge(pairs_added, 2 * (SLOTS // 2 * st.b + (s - RING) // 2 + 1))
                            act.wait_ge(scores_ready, g + 1)
                            nc.scalar.activation(probs[:, a, s % RING, HALF * half:HALF * (half + 1)],
                                                 scores_ps[:, u_bank(s, u), :], ACT.Exp,
                                                 scale=exp_scale[:, 0:1]).then_inc(probs_ready, 1)
                    if st.project_in and s in XHAT_SLOTS:
                        k = XHAT_SLOTS.index(s)
                        t, hi = divmod(k, 2)
                        if k == 0:
                            act.wait_ge(rstd_step, 2 * (st.b + 3))
                            if due(st.b + 2):
                                act.wait_ge(xlo_ready, LO * (st.b + 2))
                        to = (xhat[:, t, :], (xhat_a_hi, xhat_b)[t][:, st.parity, :])[hi]
                        nc.scalar.activation(to, x_sb[:, t, :], ACT.Identity, bias=neg_mu_rstd[:, t:t + 1],
                                             scale=rstd[:, t:t + 1]).then_inc(xhat_ready, 1)
                    for j, par, p in st.due(s, HEADS_TAKEN, TILES):
                        k = PAIRS * j + p
                        act.wait_ge(heads_done, TILES * (k + 1))
                        if due(k - 1):
                            act.wait_ge(divided, k - 1)
                        nc.scalar.copy(heads_sb[:, (par + p) % 2, :], heads_ps[:, :]).then_inc(heads_taken, 1)
                    for j, par, p in st.due(s, SUMS_TAKEN, TILES):
                        k = PAIRS * j + p
                        act.wait_ge(sums_done, 2 * (k + 1))
                        if due(k):
                            act.wait_ge(sums_spread_out, MOVE * k)
                        nc.scalar.copy(sums_sb[:, :], sums_ps[:, :]).then_inc(sums_taken, 1)
                    for j, par, p in st.due(s, DIVIDED, TILES):
                        k = PAIRS * j + p
                        act.wait_ge(divided, k + 1)
                        if due(k):
                            act.wait_ge(attn_moved, MOVE * ATTN_MOVES * k)
                        nc.scalar.copy(heads_hi[:, :], heads_out[:, :]).then_inc(heads_hi_ready, 1)
                    kind, i = st.extra(s) or (None, 0)
                    g = st.ordinal(s)
                    if kind == "qk":
                        t, half = divmod(i, 2)
                        if i == 0 and due(st.b + 2):
                            for p in range(PAIRS):
                                act.wait_ge(stacked[p], MOVE * STACK_MOVES * (st.b + 2))
                        act.wait_ge(extra_filled, g + 1)
                        nc.scalar.copy(qk_hi[:, t, HALF * half:HALF * (half + 1)],
                                       extra_ps[:, :]).then_inc(qk_hi_ready, 1)
                    elif kind == "v":
                        act.wait_ge(extra_filled, g + 1)
                        nc.scalar.copy(v_sb[:, 1 - st.parity, 2 * i:2 * i + 2, :].rearrange("p t c -> p (t c)"),
                                       extra_ps[:, 0:2 * C]).then_inc(extra_freed, 1)
                    elif kind == "proj":
                        t = i // 2
                        act.wait_ge(extra_filled, g + 1)
                        if i >= 2:
                            act.wait_ge(residual_added, 4 * (st.b - 1) + i - 1)
                        elif i == 0:
                            act.wait_ge(res_loaded, MOVE * st.b)
                        nc.scalar.activation(projected[:, i % 2, :], extra_ps[0:OM, :], ACT.Identity,
                                             bias=bias[:, t:t + 1], scale=proj_unscale[0:OM, 0:1]
                                             ).then_inc(extra_freed, 1)

            run_steps(act, step)

        @block.gpsimd
        def _(pool):
            def step(st):
                for s in range(SLOTS):
                    if st.project_in and s == VAR_SLOT:
                        pool.wait_ge(extra_freed, st.ordinal(s) + 1)
                        nc.gpsimd.tensor_tensor(rstd[:, :], var_eps[:, :], minus_half[:, :],
                                                ALU.pow).then_inc(rstd_step, 1)
                        pool.wait_ge(rstd_step, 2 * (st.b + 2) + 1)
                        nc.gpsimd.tensor_tensor(neg_mu_rstd[:, :], neg_mu[:, :], rstd[:, :],
                                                ALU.mult).then_inc(rstd_step, 1)
                    if st.project_in and s == XHAT_SLOTS[-1]:
                        pool.wait_ge(xhat_ready, XHAT * (st.b + 3))
                        nc.gpsimd.tensor_tensor(xhat_a_lo[:, st.parity, :], xhat[:, 0, :],
                                                xhat_a_hi[:, st.parity, :], ALU.subtract).then_inc(xlo_ready, 1)
                        pool.wait_ge(xlo_ready, 2 * (st.b + 2) + 1)
                        nc.gpsimd.tensor_tensor(xhat_b[CB:P, st.parity, :], xhat[CB:P, 1, :],
                                                xhat_b[CB:P, st.parity, :], ALU.subtract).then_inc(xlo_ready, 1)
                        pool.wait_ge(xlo_ready, 2 * (st.b + 3))
                    for j, par, p in st.due(s, DIVIDED + 1, TILES):
                        k = PAIRS * j + p
                        pool.wait_ge(heads_hi_ready, k + 1)
                        nc.gpsimd.tensor_tensor(heads_lo[:, :], heads_out[:, :], heads_hi[:, :],
                                                ALU.subtract).then_inc(heads_lo_ready, 1)
                    if st.tail and s - 1 in PROJ_SLOTS:
                        i = PROJ_SLOTS.index(s - 1)
                        t, half = divmod(i, 2)
                        pool.wait_ge(extra_freed, st.ordinal(s - 1) + 1)
                        if i == 0:
                            pool.wait_ge(res_loaded, MOVE * st.b)
                        n = slice(HALF * half, HALF * (half + 1))
                        nc.gpsimd.tensor_tensor(x_res[:, t, n], projected[:, i % 2, :], x_res[:, t, n],
                                                ALU.add).then_inc(residual_added, 1)
                    if st.attend and s % 2 == 1:
                        j = s // 2
                        for a in range(2):
                            pool.wait_ge(probs_ready, SCORE_UNITS * (SLOTS * st.b + s) + 2 * (a + 1))
                            q = SLOTS // QUAD * st.b + (j - PAIR_RING) // 2
                            if a == 0 and due(q + 1):
                                pool.wait_ge(sums_done, q + 1)
                            nc.gpsimd.tensor_tensor(prob_pairs[:, a, j % PAIR_RING, :],
                                                    probs[:, a, (s - 1) % RING, :],
                                                    probs[:, a, s % RING, :], ALU.add).then_inc(pairs_added, 1)

            run_steps(pool, step)

        @block.vector
        def _(dve):
            nc.vector.memset(minus_half[:, :], -0.5)
            nc.vector.memset(k_stack[STACK:SHIFTED, :, :, :], SHIFT)
            nc.vector.memset(ones[:, :], 1.0).then_inc(setup, 1)
            dve.wait_ge(const_loaded, MOVE * 14)
            for t in range(2):
                for w, absolute in ((w_f32, w_abs), (wp_f32, wp_abs)):
                    nc.vector.scalar_tensor_tensor(out=absolute[:, t, :], in0=w[:, t, :], scalar=-1.0,
                                                   in1=w[:, t, :], op0=ALU.mult,
                                                   op1=ALU.max).then_inc(setup, 1)
            dve.wait_ge(l1_ready, 1)
            nc.vector.tensor_reduce(l1_max[:, 0:3], scores_ps[:, :, 0:C], AX_X, ALU.max).then_inc(setup, 1)
            nc.vector.tensor_reduce(l1_max[:, 3:4], extra_ps[:, 0:C], AX_X, ALU.max).then_inc(setup, 1)
            dve.wait_ge(setup, 7)
            nc.vector.tensor_scalar(unscale[:, 0:3], l1_max[:, 0:3], XHAT_MAX / LIMIT, 1e-30,
                                    ALU.mult, ALU.max).then_inc(setup, 1)
            nc.vector.tensor_scalar(unscale[:, 3:4], l1_max[:, 3:4], 1.0 / PROJ_LIMIT, 1e-30,
                                    ALU.mult, ALU.max).then_inc(setup, 1)
            dve.wait_ge(setup, 9)
            nc.vector.reciprocal(rescale[:, :], unscale[:, :]).then_inc(setup, 1)
            nc.vector.tensor_scalar(exp_scale[:, :], unscale[:, 0:1], unscale[:, 1:2], SCALE,
                                    ALU.mult, ALU.mult)
            nc.vector.tensor_scalar(proj_unscale[:, :], unscale[:, 2:3], unscale[:, 3:4], None, ALU.mult)
            dve.wait_ge(setup, 10)
            for i in range(3):
                sec = slice(C * i, C * (i + 1))
                nc.vector.tensor_scalar(w_f32[:, :, sec], w_f32[:, :, sec], rescale[:, i:i + 1], None,
                                        ALU.mult).then_inc(setup, 1)
            nc.vector.tensor_scalar(wp_f32[:, :, :], wp_f32[:, :, :], rescale[:, 3:4], None,
                                    ALU.mult).then_inc(setup, 1)
            dve.wait_ge(setup, 14)
            nc.vector.tensor_copy(w_hi[:, :, :], w_f32[:, :, :]).then_inc(setup, 1)
            nc.vector.tensor_copy(wp_hi[:, :, :], wp_f32[:, :, :]).then_inc(setup, 1)
            dve.wait_ge(setup, 16)
            nc.vector.tensor_tensor(w_lo[:, :, :], w_f32[:, :, :], w_hi[:, :, :], ALU.subtract).then_inc(setup, 1)
            nc.vector.tensor_tensor(wp_lo[:, :, :], wp_f32[:, :, :], wp_hi[:, :, :],
                                    ALU.subtract).then_inc(setup, 1)

            def statistics(st):
                j = st.b + 2
                dve.wait_ge(x_loaded, MOVE * 3 * (j + 1))
                for t in range(2):
                    for half in range(HALVES):
                        nc.vector.bn_stats(half_stats[:, t, half, :],
                                           x_sb[:, t, HALF * half:HALF * (half + 1)]).then_inc(stats_step, 1)
                dve.wait_ge(stats_step, STATS * j + 4)
                dve.sem_inc(halves_seen, 1)
                for t in range(2):
                    nc.vector.bn_aggr(chan_stats[:, t, :],
                                      half_stats[:, t, :, :].rearrange("p a b -> p (a b)")).then_inc(stats_step, 1)

            def row_max(st, s, u):
                p, tile = divmod(s, TILES)
                a, half = divmod(u, 2)
                k, g = PAIRS * (st.b + 1) + p, 2 * (SLOTS * (st.b + 1) + s) + a
                dve.wait_ge(max_filled[half], g + 1)
                if tile == 0 and u == 0 and due(k):
                    dve.wait_ge(neg_max_ready, k)
                nc.vector.tensor_reduce(half_max[:, a, tile, half:half + 1], max_ps[:, half, :], AX_X,
                                        ALU.max).then_inc(max_read[half], 1)

            def read(st, s):
                kind, i = st.extra(s)
                g = st.ordinal(s)
                if kind == "shift":
                    k = PAIRS * (st.b if i == PAIRS - 1 else st.b + 1) + i
                    dve.wait_ge(extra_filled, g + 1)
                    if due(k):
                        dve.wait_ge(shift_moved, MOVE * 2 * k)
                    turned = extra_ps[0:2 * TILES, 0:P]
                    nc.vector.tensor_scalar(shift_rows[:, 0, :], turned, 1.0 / SHIFT, None,
                                            ALU.mult).then_inc(shift_step, 1)
                    dve.wait_ge(shift_step, 2 * k + 1)
                    nc.vector.scalar_tensor_tensor(out=shift_rows[:, 1, :], in0=turned, scalar=1.0 / SHIFT,
                                                   in1=shift_rows[:, 0, :], op0=ALU.mult,
                                                   op1=ALU.subtract).then_inc(shift_step, 1)
                    dve.wait_ge(shift_step, 2 * k + 2)
                    dve.sem_inc(extra_freed, 1)
                elif kind == "mean":
                    j = st.b + 2
                    dve.wait_ge(extra_filled, g + 1)
                    nc.vector.tensor_scalar(neg_mu[:, :], extra_ps[:, 0:2], -1.0, None,
                                            ALU.mult).then_inc(extra_freed, 1)
                    dve.wait_ge(extra_freed, g + 1)
                    nc.vector.tensor_tensor(mu_off[:, :], chan_stats[:, :, 0], neg_mu[:, :],
                                            ALU.add).then_inc(stats_step, 1)
                    dve.wait_ge(stats_step, STATS * j + 7)
                    nc.vector.tensor_tensor(mu_off2[:, :], mu_off[:, :], mu_off[:, :],
                                            ALU.mult).then_inc(stats_step, 1)
                    dve.wait_ge(stats_step, STATS * j + 8)
                    nc.vector.tensor_tensor(chan_var[:, :], chan_stats[:, :, 1], mu_off2[:, :],
                                            ALU.add).then_inc(stats_step, 1)
                elif kind == "var":
                    dve.wait_ge(extra_filled, g + 1)
                    nc.vector.tensor_scalar(var_eps[:, :], extra_ps[:, 0:2], EPS, None,
                                            ALU.add).then_inc(extra_freed, 1)
                elif kind == "qk":
                    t, half = divmod(i, 2)
                    n = slice(HALF * half, HALF * (half + 1))
                    dve.wait_ge(qk_hi_ready, 6 * (st.b + 2) + i + 1)
                    nc.vector.tensor_tensor(qk_lo[:, t, n], extra_ps[:, :], qk_hi[:, t, n],
                                            ALU.subtract).then_inc(extra_freed, 1)

            def add_quad(j, q, half):
                n = slice(HALF * half, HALF * (half + 1))
                for a in range(2):
                    dve.wait_ge(pairs_added, 4 * (SLOTS // QUAD * j + q) + 3 + a)
                    second = prob_pairs[:, a, (2 * q + 1) % PAIR_RING, n]
                    nc.vector.tensor_tensor(second, prob_pairs[:, a, 2 * q % PAIR_RING, n], second,
                                            ALU.add).then_inc(quads_added, 1)

            def step(st):
                for s in range(SLOTS):
                    if s == 0 and st.project_in:
                        statistics(st)
                    for u in range(SCORE_UNITS):
                        if u == 1 and s > 0 and st.extra(s - 1) is not None:
                            read(st, s - 1)
                        for half in range(HALVES):
                            if u == 2 * half + 1:
                                for j, par, q in st.due(s, QUAD_ADDED, QUAD):
                                    add_quad(j, q, half)
                        if st.maxima:
                            row_max(st, s, u)
                    for j, par, p in st.due(s, SUMS_TURNED, TILES):
                        k = PAIRS * j + p
                        dve.wait_ge(sums_spread_out, MOVE * (k + 1))
                        if due(k):
                            dve.wait_ge(inv_gathered, MOVE * k)
                        nc.vector.reciprocal(inv_spread[:, :], sums_spread[:, :]).then_inc(inverted, 1)
                    for j, par, p in st.due(s, DIVIDED, TILES):
                        k = PAIRS * j + p
                        dve.wait_ge(inv_broadcast, MOVE * 4 * (k + 1))
                        if due(k):
                            dve.wait_ge(heads_lo_ready, k)
                        nc.vector.tensor_tensor(heads_out[:, :], heads_sb[:, (par + p) % 2, :], inv_sb[:, :],
                                                ALU.mult).then_inc(divided, 1)
                    if s % TILES == TILES - 1 and st.maxima:
                        for half in range(HALVES):
                            dve.wait_ge(max_read[half], 2 * (SLOTS * (st.b + 1) + s + 1))
                        nc.vector.tensor_reduce(neg_max[:, :],
                                                half_max[:, :, :, :].rearrange("p a t h -> p (a t) h"),
                                                AX_X, ALU.max, negate=True).then_inc(neg_max_ready, 1)

            run_steps(dve, step)




def u_bank(s, u):
    return (SCORE_UNITS * s + u) % SCORE_BANKS


def kernel(x, L0_conv_qkv_w, L0_conv_proj_w, L0_conv_proj_b):
    import concourse.bacc as bacc
    from concourse.bass_utils import run_bass_kernel_spmd

    channel = np.arange(C) // GROUP
    arrays = {
        "x": np.ascontiguousarray(x).reshape(BATCH, C, N),
        "qkv_wT": np.ascontiguousarray(np.asarray(L0_conv_qkv_w).T),
        "proj_wT": np.ascontiguousarray(np.asarray(L0_conv_proj_w).T),
        "proj_b": np.ascontiguousarray(np.asarray(L0_conv_proj_b).reshape(2, OM).T),
        "group_mean": np.where(channel[:, None] == channel[None, :], np.float32(1.0 / GROUP), np.float32(0.0)),
        "identity": np.eye(P, dtype=np.float32),
    }
    nc = bacc.Bacc("TRN2", target_bir_lowering=False, num_devices=1)
    ins = [nc.dram_tensor(name, a.shape, mybir.dt.from_np(a.dtype), kind="ExternalInput").ap()
           for name, a in arrays.items()]
    out = nc.dram_tensor("out", (BATCH, C, N), F32, kind="ExternalOutput").ap()
    group_norm_attention(nc, *ins, out)
    r = run_bass_kernel_spmd(nc, [arrays], core_ids=[0])
    return r.results[0]["out"].reshape(BATCH, C, H, W)
```

```python
from contextlib import ExitStack
from math import sqrt

import numpy as np

import concourse.bass as bass
from concourse import mybir

F32 = mybir.dt.float32
F16 = mybir.dt.float16
ALU = mybir.AluOpType
ACT = mybir.ActivationFunctionType
AX_X = mybir.AxisListType.X

BATCH = 16
C = 192
H = W = 32
N = H * W
HEADS = 6
D = C // HEADS
GROUPS = 32
GROUP = C // GROUPS
EPS = 1e-5
SCALE = D ** -0.5

P = 128
HALF = 512
HALVES = N // HALF
TILES = N // P
PAIRS = HEADS // 2
SLOTS = PAIRS * TILES
CB = C - P
SCORE_UNITS = 4
SCORE_BANKS = 2
MAX_BANKS = 3
MAX_UNITS = SCORE_UNITS * SLOTS // MAX_BANKS
RING = 4
PAIR_RING = 4
OM = C // 2

STACK = 3 * D
SHIFTED = STACK + 2
SHIFT = 2.0 ** 15
LIMIT = 8192.0
XHAT_MAX = sqrt(GROUP * N)
PROJ_LIMIT = 64.0

LEAD = 12
SHIFT_SLOTS = {5: 1, 13: 2, 21: 0}
STATS_AT = ((16, 1), (16, 3), (17, 1), (17, 3))
AGGREGATE_AT = (20, 2)
MEAN_SLOT, VAR_SLOT = 0, 2
XHAT_AT = ((3, 3), (4, 1), (5, 3), (6, 1), (6, 3), (7, 3), (9, 1), (9, 3))
XLO_SLOTS = (8, 10)
QK_FIRST_SLOTS = (12, 13, 14, 15, 16, 17)
QK_SECOND_SLOTS = (17, 19, 22)
V_SECOND_SLOTS = (14, 15, 18, 20)
V_SLOTS = (7, 8, 11, 22)
QK_SLOTS = (12, 16, 19)
QK_LATE_SLOTS = (3, 4, 6)
PROJ_SLOTS = (14, 15, 18, 20)
EXTRA_SLOTS = (*SHIFT_SLOTS, MEAN_SLOT, VAR_SLOT, *V_SLOTS, *QK_SLOTS, *QK_LATE_SLOTS, *PROJ_SLOTS)
assert len(set(EXTRA_SLOTS)) == len(EXTRA_SLOTS)
STACK_SLOTS = {7: 0, 9: 1, 11: 2}
LOAD_SLOT = 10
HEADS_TAKEN = TILES
SUMS_TAKEN = TILES + 5
SUMS_SPREAD = TILES + 6
INVERTED = TILES + 7
INV_SPREAD = TILES + 8
DIVIDED = TILES + 9
MOVED = (23, 20, 20)
QUAD = 4
QUAD_ADDED = QUAD + 2
QUAD_COUNTED = QUAD + 5
COUNT_UNIT, HEADS_UNIT, SUMS_UNIT = 3, 2, 3

STATS = 9
XHAT = 8
LO = 2
MOVE = 16
ATTN_MOVES = 4
STACK_MOVES = 6


class Step:

    def __init__(self, b, at, extras):
        self.b = b
        self.parity = at % 2
        self.attend = 0 <= at < BATCH
        self.follow = 0 <= at + 1 < BATCH
        self.project_in = 0 <= at + 2 < BATCH
        self.take_stats = 0 <= at + 3 < BATCH
        self.tail = 0 <= at - 1 < BATCH
        self.qk_slots = {-2: QK_FIRST_SLOTS, -1: QK_SECOND_SLOTS}.get(at, QK_SLOTS)
        self.v_slots = V_SECOND_SLOTS if at == -1 else V_SLOTS
        self.late = at >= 0 and self.follow
        self.extras = extras

    def extra(self, s):
        if s in SHIFT_SLOTS and (self.follow if SHIFT_SLOTS[s] == 0 else self.attend):
            return "shift", SHIFT_SLOTS[s]
        if self.project_in and s in (MEAN_SLOT, VAR_SLOT):
            return ("mean", 0) if s == MEAN_SLOT else ("var", 0)
        if self.follow and s in self.v_slots:
            return "v", self.v_slots.index(s)
        if self.project_in and s in self.qk_slots:
            return "qk", self.qk_slots.index(s)
        if self.late and s in QK_LATE_SLOTS:
            return "qk", len(QK_SLOTS) + QK_LATE_SLOTS.index(s)
        if self.tail and s in PROJ_SLOTS:
            return "proj", PROJ_SLOTS.index(s)
        return None

    def maxed(self, s):
        if s < SLOTS - LEAD:
            return (self.b, self.parity, s + LEAD) if self.attend else None
        return (self.b + 1, 1 - self.parity, s + LEAD - SLOTS) if self.follow else None

    def shifted(self, pair):
        return (self.b + 1, 1 - self.parity) if pair == 0 else (self.b, self.parity)

    def made(self, i):
        return (self.b + 2, self.parity) if i < len(self.qk_slots) else (self.b + 1, 1 - self.parity)

    def ordinal(self, slot):
        return self.extras + sum(self.extra(s) is not None for s in range(slot))

    def due(self, s, offset, every):
        at = s - offset
        if at % every == 0 and at >= 0 and self.attend:
            return [(self.b, self.parity, at // every)]
        if at % every == 0 and -SLOTS <= at < 0 and self.tail:
            return [(self.b - 1, 1 - self.parity, (at + SLOTS) // every)]
        return []

    def moved(self, s):
        return [x for p in range(PAIRS) for x in self.due(s, MOVED[p], TILES) if x[2] == p]


SPREAD = 4 * HALF // P
SETUP = 19

LOOP_FIRST, LOOP_END = 1, 13


def run_steps(eng, step):
    extras = 0
    for at in range(-3, LOOP_FIRST):
        st = Step(at, at, extras)
        step(st)
        extras = st.ordinal(SLOTS)
    per = Step(LOOP_FIRST, LOOP_FIRST, 0).ordinal(SLOTS)
    with eng.Fori(0, (LOOP_END - LOOP_FIRST) // 2) as i:
        for k in range(2):
            step(Step(2 * i + (LOOP_FIRST + k), LOOP_FIRST + k, 2 * per * i + (extras + per * k)))
    extras += per * (LOOP_END - LOOP_FIRST)
    for at in range(LOOP_END, BATCH + 1):
        st = Step(at, at, extras)
        step(st)
        extras = st.ordinal(SLOTS)


def due(count):
    return not isinstance(count, int) or count > 0


def group_norm_attention(nc, x, qkv_wT, proj_wT, proj_b, group_mean, identity, out):
    with ExitStack() as ctx:
        def sb(name, shape, dt):
            return ctx.enter_context(nc.sbuf_tensor(name, shape, dt))

        def psum(name, shape):
            return ctx.enter_context(nc.psum_tensor(name, shape, F32))

        def sem(name):
            return ctx.enter_context(nc.semaphore(name))

        scores_ps = psum("scores_ps", [P, SCORE_BANKS, HALF])
        max_ps = psum("max_ps", [P, MAX_BANKS, HALF])
        extra_ps = psum("extra_ps", [P, HALF])
        heads_ps = psum("heads_ps", [P, HALF])
        sums_ps = psum("sums_ps", [P, HALF])

        q_stack = sb("q_stack", [P, 2, HEADS, N], F16)
        k_stack = sb("k_stack", [P, 2, HEADS, N], F16)
        v_sb = sb("v_sb", [P, 2, TILES, C], F32)
        probs = sb("probs", [P, 2, RING, N], F32)
        prob_pairs = sb("prob_pairs", [P, 2, PAIR_RING, N], F32)
        xhat_a_hi = sb("xhat_a_hi", [P, 2, N], F16)
        xhat_a_lo = sb("xhat_a_lo", [P, 2, N], F16)
        xhat_b = sb("xhat_b", [P, 2, N], F16)
        xhat = sb("xhat", [P, 2, N], F32)
        x_sb = sb("x_sb", [P, 2, N], F32)
        qk_hi = sb("qk_hi", [P, 3, N], F16)
        qk_lo = sb("qk_lo", [P, 3, N], F16)
        heads_sb = sb("heads_sb", [P, 2, HALF], F32)
        sums_sb = sb("sums_sb", [P, HALF], F32)
        sums_spread = sb("sums_spread", [P, SPREAD], F32)
        inv_spread = sb("inv_spread", [P, SPREAD], F32)
        inv_rows = nc.dram_tensor("inv_rows", (4, HALF), F32, kind="Internal").ap()
        inv_sb = sb("inv_sb", [P, HALF], F32)
        heads_out = sb("heads_out", [P, HALF], F32)
        heads_hi = sb("heads_hi", [P, HALF], F16)
        heads_lo = sb("heads_lo", [P, HALF], F16)
        attn_a_hi = sb("attn_a_hi", [P, N], F16)
        attn_a_lo = sb("attn_a_lo", [P, N], F16)
        attn_b = sb("attn_b", [P, N], F16)
        x_res = sb("x_res", [OM, 2, N], F32)
        projected = sb("projected", [OM, 2, HALF], F32)

        w_f32 = prob_pairs[:, 0, 0:2, 0:3 * C]
        wp_f32 = prob_pairs[:, 0, 2:4, 0:C]
        w_abs = prob_pairs[:, 1, 0:2, 0:3 * C]
        wp_abs = prob_pairs[:, 1, 2:4, 0:C]
        w_hi = sb("w_hi", [P, 2, 3 * C], F16)
        w_lo = sb("w_lo", [P, 2, 3 * C], F16)
        wp_hi = sb("wp_hi", [P, 2, C], F16)
        wp_lo = sb("wp_lo", [P, 2, C], F16)
        bias = sb("bias", [OM, 2], F32)
        mean_a = sb("mean_a", [P, 2, P], F32)
        mean_b = sb("mean_b", [CB, 2, P], F32)
        ident = sb("ident", [P, P], F32)
        ones = sb("ones", [P, P], F32)
        l1_max = sb("l1_max", [P, 4], F32)
        unscale = sb("unscale", [P, 4], F32)
        rescale = sb("rescale", [P, 4], F32)
        proj_unscale = sb("proj_unscale", [P, 1], F32)
        exp_scale = sb("exp_scale", [P, 1], F32)

        half_stats = sb("half_stats", [P, 2, HALVES, 6], F32)
        chan_stats = sb("chan_stats", [P, 2, 2], F32)
        neg_mu = sb("neg_mu", [P, 2], F32)
        mu_off = sb("mu_off", [P, 2], F32)
        mu_off2 = sb("mu_off2", [P, 2], F32)
        chan_var = sb("chan_var", [P, 2], F32)
        var_eps = sb("var_eps", [P, 2], F32)
        minus_half = sb("minus_half", [P, 2], F32)
        rstd = sb("rstd", [P, 2], F32)
        neg_mu_rstd = sb("neg_mu_rstd", [P, 2], F32)
        half_max = sb("half_max", [P, 2, TILES, HALVES], F32)
        neg_max = sb("neg_max", [P, 2 * TILES], F32)
        shift_rows = sb("shift_rows", [2 * TILES, 2, P], F16)

        const_loaded = sem("const_loaded")
        setup = sem("setup")
        l1_ready = sem("l1_ready")
        shift_set = sem("shift_set")
        x_loaded = sem("x_loaded")
        stats_step = sem("stats_step")
        halves_seen = sem("halves_seen")
        rstd_step = sem("rstd_step")
        xhat_ready = sem("xhat_ready")
        xlo_ready = sem("xlo_ready")
        max_filled = [sem(f"max_filled{i}") for i in range(MAX_BANKS)]
        max_read = [sem(f"max_read{i}") for i in range(MAX_BANKS)]
        extra_filled = sem("extra_filled")
        extra_freed = sem("extra_freed")
        qk_hi_ready = sem("qk_hi_ready")
        stacked = [sem(f"stacked{p}") for p in range(PAIRS)]
        neg_max_ready = sem("neg_max_ready")
        shift_step = sem("shift_step")
        shift_moved = sem("shift_moved")
        scores_ready = sem("scores_ready")
        probs_ready = sem("probs_ready")
        pairs_added = sem("pairs_added")
        heads_done = sem("heads_done")
        sums_done = sem("sums_done")
        quads_added = sem("quads_added")
        heads_taken = sem("heads_taken")
        sums_taken = sem("sums_taken")
        sums_spread_out = sem("sums_spread_out")
        inverted = sem("inverted")
        inv_gathered = sem("inv_gathered")
        inv_broadcast = sem("inv_broadcast")
        divided = sem("divided")
        heads_hi_ready = sem("heads_hi_ready")
        heads_lo_ready = sem("heads_lo_ready")
        proj_taken = sem("proj_taken")
        residual_added = sem("residual_added")
        attn_moved = sem("attn_moved")
        res_loaded = sem("res_loaded")
        y_stored = sem("y_stored")

        block = ctx.enter_context(nc.Block())

        @block.sync
        def _(sp):
            sp.dma_start(w_f32[:, 0, :], qkv_wT[0:P, :]).then_inc(const_loaded, MOVE)
            for r in range(2):
                sp.dma_start(w_f32[CB * r:CB * (r + 1), 1, :], qkv_wT[P:C, :]).then_inc(const_loaded, MOVE)
            sp.dma_start(wp_f32[:, 0, :], proj_wT[0:P, :]).then_inc(const_loaded, MOVE)
            for r in range(2):
                sp.dma_start(wp_f32[CB * r:CB * (r + 1), 1, :], proj_wT[P:C, :]).then_inc(const_loaded, MOVE)
            sp.dma_start(bias[:, :], proj_b).then_inc(const_loaded, MOVE)
            sp.dma_start(ident[:, :], identity).then_inc(const_loaded, MOVE)
            sp.dma_start(mean_a[:, 0, :], group_mean[0:P, 0:P]).then_inc(const_loaded, MOVE)
            sp.dma_start(mean_b[:, 0, :], group_mean[P:C, 0:P]).then_inc(const_loaded, MOVE)
            for r in range(2):
                to = slice(CB * r, CB * (r + 1))
                sp.dma_start(mean_a[:, 1, to], group_mean[0:P, P:C]).then_inc(const_loaded, MOVE)
                sp.dma_start(mean_b[:, 1, to], group_mean[P:C, P:C]).then_inc(const_loaded, MOVE)

            def load_x(j):
                sp.dma_start(x_sb[:, 0, :], x[j, 0:P, :]).then_inc(x_loaded, MOVE)
                for r in range(2):
                    sp.dma_start(x_sb[CB * r:CB * (r + 1), 1, :], x[j, P:C, :]).then_inc(x_loaded, MOVE)

            load_x(0)
            sp.sem_inc(y_stored, MOVE)

            def stack_pair(par, p):
                for stack, row, parts in ((q_stack, 2 * D * p, (qk_hi, qk_lo, qk_hi)),
                                          (k_stack, C + 2 * D * p, (qk_hi, qk_hi, qk_lo))):
                    for n, part in enumerate(parts):
                        sp.dma_start(stack[D * n:D * (n + 1), par, 2 * p:2 * p + 2, :],
                                     part[row % P:row % P + 2 * D, row // P, :]).then_inc(stacked[p], MOVE)

            def step(st):
                b = st.b
                for s in range(SLOTS):
                    if s == QK_FIRST_SLOTS[-1] + 1 and not st.follow and st.project_in:
                        sp.wait_ge(extra_freed, st.ordinal(s))
                        for p in range(PAIRS):
                            stack_pair(st.parity, p)
                    if s in STACK_SLOTS and st.late:
                        sp.wait_ge(extra_freed, st.ordinal(QK_LATE_SLOTS[-1]) + 1)
                        stack_pair(1 - st.parity, STACK_SLOTS[s])
                    if s > 0 and st.extra(s - 1) is not None and st.extra(s - 1)[0] == "shift":
                        p = st.extra(s - 1)[1]
                        j, par = st.shifted(p)
                        sp.wait_ge(shift_step, 2 * (PAIRS * j + p + 1))
                        for part in range(2):
                            sp.dma_start(q_stack[STACK + part:STACK + part + 1, par, 2 * p:2 * p + 2, :],
                                         shift_rows[:, part, :]).then_inc(shift_moved, MOVE)
                    for j, par, p in st.due(s, SUMS_SPREAD, TILES):
                        k = PAIRS * j + p
                        sp.wait_ge(sums_taken, k + 1)
                        sp.dma_start(sums_spread[:, :], sums_sb[0:P:D, :]
                                     ).then_inc(sums_spread_out, MOVE)
                    for j, par, p in st.due(s, INV_SPREAD, TILES):
                        k = PAIRS * j + p
                        sp.wait_ge(inverted, k + 1)
                        sp.dma_start(inv_rows[:, :].rearrange("g (q n) -> (g q) n", n=SPREAD),
                                     inv_spread[:, :]).then_inc(inv_gathered, MOVE)
                        sp.wait_ge(inv_gathered, MOVE * (k + 1))
                        sp.dma_start(inv_sb[:, :], inv_rows[:, :].unsqueeze(1).broadcast_to([4, D, HALF])
                                     ).then_inc(inv_broadcast, MOVE)
                    for j, par, p in st.moved(s):
                        if p == 0 and st.tail:
                            sp.wait_ge(residual_added, 4 * b)
                        else:
                            sp.wait_ge(heads_lo_ready, PAIRS * j + p + 1)
                        for half in range(HALVES):
                            n, rows = slice(HALF * half, HALF * (half + 1)), slice(2 * D * half, 2 * D * (half + 1))
                            for lo, (to, row) in enumerate((((attn_a_hi, 0), (attn_a_lo, 0)),
                                                            ((attn_a_hi, 2 * D), (attn_a_lo, 2 * D)),
                                                            ((attn_b, 0), (attn_b, 2 * D)))[p]):
                                sp.dma_start(to[row:row + 2 * D, n],
                                             (heads_hi, heads_lo)[lo][rows, :]).then_inc(attn_moved, MOVE)
                    if s == 4 and st.tail:
                        sp.wait_ge(y_stored, MOVE * b)
                        sp.dma_start(x_res[:, :, :],
                                     x[b - 1, :, :].rearrange("(t p) n -> p t n", p=OM)).then_inc(res_loaded, MOVE)
                    if s == LOAD_SLOT and st.project_in and not (isinstance(b, int) and b + 3 >= BATCH):
                        sp.wait_ge(xhat_ready, XHAT * (b + 3))
                        load_x(b + 3)
                    if s == SLOTS - 1 and st.tail:
                        sp.wait_ge(residual_added, 4 * b)
                        sp.dma_start(out[b - 1, :, :].rearrange("(t p) n -> p t n", p=OM),
                                     x_res[:, :, :]).then_inc(y_stored, MOVE)

            run_steps(sp, step)
            sp.wait_ge(y_stored, MOVE * (BATCH + 1))

        @block.tensor
        def _(pe):
            pe.wait_ge(setup, 5)
            for i in range(4):
                ps = extra_ps[:, 0:C] if i == 3 else (scores_ps[:, i, 0:C] if i < 2 else max_ps[:, 0, 0:C])
                w = (wp_abs[:, :, :] if i == 3 else w_abs[:, :, C * i:C * (i + 1)])
                pe.matmul(ps, ones[:, :], w[:, 0, :], start=True, stop=False)
                last = pe.matmul(ps, ones[0:CB, :], w[0:CB, 1, :], start=False, stop=True)
            last.then_inc(l1_ready, 1)

            def row_max(st, s, u):
                j, par, s = st.maxed(s)
                p, tile = divmod(s, TILES)
                a, half = divmod(u, 2)
                h = 2 * p + a
                turn, bank = divmod(SCORE_UNITS * s + u, MAX_BANKS)
                g = MAX_UNITS * j + turn
                if tile == 0 and u == 0:
                    pe.wait_ge(stacked[p], MOVE * STACK_MOVES * (j + 1))
                if due(g):
                    pe.wait_ge(max_read[bank], g)
                pe.matmul(max_ps[:, bank, :], q_stack[0:STACK, par, h, P * tile:P * (tile + 1)],
                          k_stack[0:STACK, par, h, HALF * half:HALF * (half + 1)],
                          start=True, stop=True).then_inc(max_filled[bank], 1)

            def fill(st, s, part):
                kind, i = st.extra(s)
                g = st.ordinal(s)
                if part == 0 and due(g):
                    pe.wait_ge(extra_freed, g)
                last = None
                if kind == "shift" and part == 0:
                    pe.wait_ge(neg_max_ready, PAIRS * st.shifted(i)[0] + i + 1)
                    last = pe.transpose(extra_ps[0:2 * TILES, 0:P], neg_max[:, :], ident[:, :])
                elif kind in ("mean", "var") and part == 0:
                    pe.wait_ge(stats_step, STATS * (st.b + 2) + (6 if kind == "mean" else 9))
                    for t in range(2):
                        per_chan = (chan_stats[:, 0, 0:1], chan_stats[0:CB, 1, 0:1]) if kind == "mean" else \
                            (chan_var[:, 0:1], chan_var[0:CB, 1:2])
                        pe.matmul(extra_ps[:, t:t + 1], mean_a[:, t, :], per_chan[0], start=True, stop=False)
                        last = pe.matmul(extra_ps[:, t:t + 1], mean_b[:, t, :], per_chan[1],
                                         start=False, stop=True)
                elif kind == "qk":
                    t, half = divmod(i, 2)
                    j, par = st.made(i)
                    if i == 0 and part == 0:
                        pe.wait_ge(xlo_ready, LO * (j + 1))
                    o, n = slice(P * t, P * (t + 1)), slice(HALF * half, HALF * (half + 1))
                    last = product(part, extra_ps[:, :], w_hi[:, :, o], w_lo[:, :, o], xhat_a_hi[:, par, n],
                                   xhat_a_lo[:, par, n], xhat_b[:, par, n])
                elif kind == "v":
                    par, o = 1 - st.parity, slice(2 * C, 3 * C)
                    n = slice(P * (2 * i + part), P * (2 * i + part + 1))
                    to = extra_ps[:, C * part:C * (part + 1)]
                    pe.matmul(to, xhat_a_hi[:, par, n], w_hi[:, 0, o], start=True, stop=False)
                    pe.matmul(to, xhat_a_hi[:, par, n], w_lo[:, 0, o], start=False, stop=False)
                    pe.matmul(to, xhat_a_lo[:, par, n], w_hi[:, 0, o], start=False, stop=False)
                    pe.matmul(to, xhat_b[:, par, n], w_hi[:, 1, o], start=False, stop=False)
                    second = pe.matmul(to, xhat_b[0:CB, par, n], w_lo[0:CB, 1, o], start=False, stop=True)
                    last = second if part == 1 else None
                elif kind == "proj":
                    t, half = divmod(i, 2)
                    if i == 0 and part == 0:
                        pe.wait_ge(attn_moved, MOVE * ATTN_MOVES * PAIRS * st.b)
                    o, n = slice(OM * t, OM * (t + 1)), slice(HALF * half, HALF * (half + 1))
                    last = product(part, extra_ps[0:OM, :], wp_hi[:, :, o], wp_lo[:, :, o], attn_a_hi[:, n],
                                   attn_a_lo[:, n], attn_b[:, n])
                if last is not None:
                    last.then_inc(extra_filled, 1)

            def product(part, to, hi, lo, a_hi, a_lo, b):
                if part == 0:
                    pe.matmul(to, hi[:, 0, :], a_hi, start=True, stop=False)
                    pe.matmul(to, lo[:, 0, :], a_hi, start=False, stop=False)
                    pe.matmul(to, hi[:, 0, :], a_lo, start=False, stop=False)
                    return None
                pe.matmul(to, hi[:, 1, :], b, start=False, stop=False)
                return pe.matmul(to, lo[0:CB, 1, :], b[0:CB, :], start=False, stop=True)

            def score(st, s, u):
                p, tile = divmod(s, TILES)
                a, half = divmod(u, 2)
                h, g = 2 * p + a, SCORE_UNITS * (SLOTS * st.b + s) + u
                if tile == 0 and u == 0:
                    pe.wait_ge(shift_moved, MOVE * 2 * (PAIRS * st.b + p + 1))
                if due(g - SCORE_BANKS + 1):
                    pe.wait_ge(probs_ready, g - SCORE_BANKS + 1)
                pe.matmul(scores_ps[:, u_bank(s, u), :],
                          k_stack[0:SHIFTED, st.parity, h, P * tile:P * (tile + 1)],
                          q_stack[0:SHIFTED, st.parity, h, HALF * half:HALF * (half + 1)],
                          start=True, stop=True).then_inc(scores_ready, 1)

            def weigh(b, par, s):
                p, tile = divmod(s, TILES)
                pe.wait_ge(probs_ready, SCORE_UNITS * (SLOTS * b + s + 1))
                if tile == 0 and due(PAIRS * b + p):
                    pe.wait_ge(heads_taken, PAIRS * b + p)
                for half in range(HALVES):
                    for a in range(2):
                        at, h = D * (2 * half + a), 2 * p + a
                        last = pe.matmul(heads_ps[at:at + D, :],
                                         v_sb[:, par, tile, D * h:D * (h + 1)],
                                         probs[:, a, s % RING, HALF * half:HALF * (half + 1)],
                                         start=(tile == 0), stop=(tile == TILES - 1))
                last.then_inc(heads_done, 1)

            def count(b, q):
                p, first = divmod(q, 2)
                pe.wait_ge(quads_added, 4 * (SLOTS // QUAD * b + q + 1))
                if first == 0 and due(PAIRS * b + p):
                    pe.wait_ge(sums_taken, PAIRS * b + p)
                for half in range(HALVES):
                    for a in range(2):
                        at = D * (2 * half + a)
                        last = pe.matmul(sums_ps[at:at + D, :], ones[:, 0:D],
                                         prob_pairs[:, a, (2 * q + 1) % PAIR_RING, HALF * half:HALF * (half + 1)],
                                         start=(first == 0), stop=(first == 1))
                last.then_inc(sums_done, 1)

            pe.wait_ge(setup, SETUP)
            pe.wait_ge(shift_set, 1)

            def step(st):
                for s in range(SLOTS):
                    for u in range(SCORE_UNITS):
                        if st.attend:
                            score(st, s, u)
                        if u == 1:
                            if s == 0 and st.tail:
                                weigh(st.b - 1, 1 - st.parity, SLOTS - 1)
                            elif s > 0 and st.attend:
                                weigh(st.b, st.parity, s - 1)
                        if u >= 2 and st.extra(s) is not None:
                            fill(st, s, u - 2)
                        if u == COUNT_UNIT:
                            for j, par, q in st.due(s, QUAD_COUNTED, QUAD):
                                count(j, q)
                        if st.maxed(s) is not None:
                            row_max(st, s, u)

            run_steps(pe, step)

        @block.scalar
        def _(act):
            def take(st, s):
                kind, i = s > 0 and st.extra(s - 1) or (None, 0)
                if kind in ("qk", "v", "proj"):
                    g = st.ordinal(s - 1)
                    act.wait_ge(extra_filled, g + 1)
                if kind == "qk":
                    t, half = divmod(i, 2)
                    if i == 0 and due(st.b + 2):
                        for p in range(PAIRS):
                            act.wait_ge(stacked[p], MOVE * STACK_MOVES * (st.b + 2))
                    nc.scalar.copy(qk_hi[:, t, HALF * half:HALF * (half + 1)],
                                   extra_ps[:, :]).then_inc(qk_hi_ready, 1)
                elif kind == "v":
                    nc.scalar.copy(v_sb[:, 1 - st.parity, 2 * i:2 * i + 2, :].rearrange("p t c -> p (t c)"),
                                   extra_ps[:, 0:2 * C]).then_inc(extra_freed, 1)
                elif kind == "proj":
                    if i >= 2:
                        act.wait_ge(residual_added, 4 * (st.b - 1) + i - 1)
                    elif i == 0:
                        act.wait_ge(res_loaded, MOVE * st.b)
                    nc.scalar.activation(projected[:, i % 2, :], extra_ps[0:OM, :], ACT.Identity,
                                         bias=bias[:, i // 2:i // 2 + 1], scale=proj_unscale[0:OM, 0:1]
                                         ).then_inc(extra_freed, 1)

            def split_heads(st, s):
                for j, par, p in st.due(s, DIVIDED + 1, TILES):
                    k = PAIRS * j + p
                    act.wait_ge(divided, k + 1)
                    if due(k):
                        act.wait_ge(attn_moved, MOVE * ATTN_MOVES * k)
                    nc.scalar.copy(heads_hi[:, :], heads_out[:, :]).then_inc(heads_hi_ready, 1)

            def normalise(st, k):
                t, hi, half = k // 4, k // 2 % 2, k % 2
                if k == 0:
                    act.wait_ge(rstd_step, 2 * (st.b + 3))
                    if due(st.b + 2):
                        act.wait_ge(xlo_ready, LO * (st.b + 2))
                n = slice(HALF * half, HALF * (half + 1))
                to = (xhat[:, t, n], (xhat_a_hi, xhat_b)[t][:, st.parity, n])[hi]
                nc.scalar.activation(to, x_sb[:, t, n], ACT.Identity, bias=neg_mu_rstd[:, t:t + 1],
                                     scale=rstd[:, t:t + 1]).then_inc(xhat_ready, 1)

            def copy_heads(st, s):
                for j, par, p in st.due(s, HEADS_TAKEN, TILES):
                    k = PAIRS * j + p
                    act.wait_ge(heads_done, TILES * (k + 1))
                    if due(k - 1):
                        act.wait_ge(divided, k - 1)
                    nc.scalar.copy(heads_sb[:, (par + p) % 2, :], heads_ps[:, :]).then_inc(heads_taken, 1)

            def copy_sums(st, s):
                for j, par, p in st.due(s, SUMS_TAKEN, TILES):
                    k = PAIRS * j + p
                    act.wait_ge(sums_done, 2 * (k + 1))
                    if due(k):
                        act.wait_ge(sums_spread_out, MOVE * k)
                    nc.scalar.copy(sums_sb[:, :], sums_ps[:, :]).then_inc(sums_taken, 1)

            def between(st, s, u):
                if u == 1:
                    split_heads(st, s)
                if st.project_in and (s, u) in XHAT_AT:
                    normalise(st, XHAT_AT.index((s, u)))
                if u == HEADS_UNIT:
                    copy_heads(st, s)
                if u == SUMS_UNIT:
                    copy_sums(st, s)

            def step(st):
                for s in range(SLOTS):
                    take(st, s)
                    if st.attend:
                        for u in range(SCORE_UNITS):
                            a, half = divmod(u, 2)
                            g = SCORE_UNITS * (SLOTS * st.b + s) + u
                            if u == 0 and due(SLOTS * st.b + s - RING + 1):
                                act.wait_ge(heads_done, SLOTS * st.b + s - RING + 1)
                                act.wait_ge(pairs_added, 2 * (SLOTS // 2 * st.b + (s - RING) // 2 + 1))
                            act.wait_ge(scores_ready, g + 1)
                            nc.scalar.activation(probs[:, a, s % RING, HALF * half:HALF * (half + 1)],
                                                 scores_ps[:, u_bank(s, u), :], ACT.Exp,
                                                 scale=exp_scale[:, 0:1]).then_inc(probs_ready, 1)
                            between(st, s, u)
                    else:
                        for u in range(SCORE_UNITS):
                            between(st, s, u)

            run_steps(act, step)

        @block.gpsimd
        def _(pool):
            nc.gpsimd.memset(k_stack[STACK:SHIFTED, :, :, :], SHIFT).then_inc(shift_set, 1)

            def step(st):
                for s in range(SLOTS):
                    if st.project_in and s == VAR_SLOT:
                        pool.wait_ge(extra_freed, st.ordinal(s) + 1)
                        nc.gpsimd.tensor_tensor(rstd[:, :], var_eps[:, :], minus_half[:, :],
                                                ALU.pow).then_inc(rstd_step, 1)
                        pool.wait_ge(rstd_step, 2 * (st.b + 2) + 1)
                        nc.gpsimd.tensor_tensor(neg_mu_rstd[:, :], neg_mu[:, :], rstd[:, :],
                                                ALU.mult).then_inc(rstd_step, 1)
                    if st.project_in and s == XLO_SLOTS[0]:
                        pool.wait_ge(xhat_ready, XHAT * (st.b + 2) + XHAT // 2)
                        nc.gpsimd.tensor_tensor(xhat_a_lo[:, st.parity, :], xhat[:, 0, :],
                                                xhat_a_hi[:, st.parity, :], ALU.subtract).then_inc(xlo_ready, 1)
                    if st.project_in and s == XLO_SLOTS[1]:
                        pool.wait_ge(xhat_ready, XHAT * (st.b + 3))
                        if st.attend:
                            pool.wait_ge(pairs_added, 2 * (SLOTS // 2 * st.b + s // 2))
                        else:
                            pool.wait_ge(xlo_ready, 2 * (st.b + 2) + 1)
                        nc.gpsimd.tensor_tensor(xhat_b[CB:P, st.parity, :], xhat[CB:P, 1, :],
                                                xhat_b[CB:P, st.parity, :], ALU.subtract).then_inc(xlo_ready, 1)
                        pool.wait_ge(xlo_ready, 2 * (st.b + 3))
                    for j, par, p in st.due(s, DIVIDED, TILES):
                        k = PAIRS * j + p
                        pool.wait_ge(inv_broadcast, MOVE * (k + 1))
                        if due(k):
                            pool.wait_ge(heads_lo_ready, k)
                        nc.gpsimd.tensor_tensor(heads_out[:, :], heads_sb[:, (par + p) % 2, :], inv_sb[:, :],
                                                ALU.mult).then_inc(divided, 1)
                    for j, par, p in st.due(s, DIVIDED + 2, TILES):
                        k = PAIRS * j + p
                        pool.wait_ge(heads_hi_ready, k + 1)
                        nc.gpsimd.tensor_tensor(heads_lo[:, :], heads_out[:, :], heads_hi[:, :],
                                                ALU.subtract).then_inc(heads_lo_ready, 1)
                    if st.tail and s - 1 in PROJ_SLOTS:
                        i = PROJ_SLOTS.index(s - 1)
                        t, half = divmod(i, 2)
                        pool.wait_ge(extra_freed, st.ordinal(s - 1) + 1)
                        if i == 0:
                            pool.wait_ge(res_loaded, MOVE * st.b)
                        n = slice(HALF * half, HALF * (half + 1))
                        nc.gpsimd.tensor_tensor(x_res[:, t, n], projected[:, i % 2, :], x_res[:, t, n],
                                                ALU.add).then_inc(residual_added, 1)
                    if st.attend and s % 2 == 1:
                        j = s // 2
                        for a in range(2):
                            pool.wait_ge(probs_ready, SCORE_UNITS * (SLOTS * st.b + s) + 2 * (a + 1))
                            q = SLOTS // QUAD * st.b + (j - PAIR_RING) // 2
                            if a == 0 and j % 2 == 0 and due(q + 1):
                                pool.wait_ge(quads_added, 4 * (q + 1))
                            elif a == 0 and due(q + 1):
                                pool.wait_ge(sums_done, q + 1)
                            nc.gpsimd.tensor_tensor(prob_pairs[:, a, j % PAIR_RING, :],
                                                    probs[:, a, (s - 1) % RING, :],
                                                    probs[:, a, s % RING, :], ALU.add).then_inc(pairs_added, 1)

            run_steps(pool, step)

        @block.vector
        def _(dve):
            nc.vector.memset(minus_half[:, :], -0.5)
            nc.vector.memset(ones[:, :], 1.0).then_inc(setup, 1)
            dve.wait_ge(const_loaded, MOVE * 14)
            for t in range(2):
                for w, absolute in ((w_f32, w_abs), (wp_f32, wp_abs)):
                    nc.vector.scalar_tensor_tensor(out=absolute[:, t, :], in0=w[:, t, :], scalar=-1.0,
                                                   in1=w[:, t, :], op0=ALU.mult,
                                                   op1=ALU.max).then_inc(setup, 1)
            dve.wait_ge(l1_ready, 1)
            nc.vector.tensor_reduce(l1_max[:, 0:2], scores_ps[:, 0:2, 0:C], AX_X, ALU.max).then_inc(setup, 1)
            nc.vector.tensor_reduce(l1_max[:, 2:3], max_ps[:, 0, 0:C], AX_X, ALU.max).then_inc(setup, 1)
            nc.vector.tensor_reduce(l1_max[:, 3:4], extra_ps[:, 0:C], AX_X, ALU.max).then_inc(setup, 1)
            dve.wait_ge(setup, 8)
            nc.vector.tensor_scalar(unscale[:, 0:3], l1_max[:, 0:3], XHAT_MAX / LIMIT, 1e-30,
                                    ALU.mult, ALU.max).then_inc(setup, 1)
            nc.vector.tensor_scalar(unscale[:, 3:4], l1_max[:, 3:4], 1.0 / PROJ_LIMIT, 1e-30,
                                    ALU.mult, ALU.max).then_inc(setup, 1)
            dve.wait_ge(setup, 10)
            nc.vector.reciprocal(rescale[:, :], unscale[:, :]).then_inc(setup, 1)
            nc.vector.tensor_scalar(exp_scale[:, :], unscale[:, 0:1], unscale[:, 1:2], SCALE,
                                    ALU.mult, ALU.mult)
            nc.vector.tensor_scalar(proj_unscale[:, :], unscale[:, 2:3], unscale[:, 3:4], None, ALU.mult)
            dve.wait_ge(setup, 11)
            for i in range(3):
                sec = slice(C * i, C * (i + 1))
                nc.vector.tensor_scalar(w_f32[:, :, sec], w_f32[:, :, sec], rescale[:, i:i + 1], None,
                                        ALU.mult).then_inc(setup, 1)
            nc.vector.tensor_scalar(wp_f32[:, :, :], wp_f32[:, :, :], rescale[:, 3:4], None,
                                    ALU.mult).then_inc(setup, 1)
            dve.wait_ge(setup, 15)
            nc.vector.tensor_copy(w_hi[:, :, :], w_f32[:, :, :]).then_inc(setup, 1)
            nc.vector.tensor_copy(wp_hi[:, :, :], wp_f32[:, :, :]).then_inc(setup, 1)
            dve.wait_ge(setup, 17)
            nc.vector.tensor_tensor(w_lo[:, :, :], w_f32[:, :, :], w_hi[:, :, :], ALU.subtract).then_inc(setup, 1)
            nc.vector.tensor_tensor(wp_lo[:, :, :], wp_f32[:, :, :], wp_hi[:, :, :],
                                    ALU.subtract).then_inc(setup, 1)

            def half_statistics(st, n):
                t, half = divmod(n, 2)
                if n == 0:
                    dve.wait_ge(x_loaded, MOVE * 3 * (st.b + 4))
                nc.vector.bn_stats(half_stats[:, t, half, :],
                                   x_sb[:, t, HALF * half:HALF * (half + 1)]).then_inc(stats_step, 1)

            def statistics(st):
                dve.wait_ge(stats_step, STATS * (st.b + 3) + 4)
                dve.sem_inc(halves_seen, 1)
                for t in range(2):
                    nc.vector.bn_aggr(chan_stats[:, t, :],
                                      half_stats[:, t, :, :].rearrange("p a b -> p (a b)")).then_inc(stats_step, 1)

            def row_max(st, s, u):
                j, par, s = st.maxed(s)
                p, tile = divmod(s, TILES)
                a, half = divmod(u, 2)
                k = PAIRS * j + p
                turn, bank = divmod(SCORE_UNITS * s + u, MAX_BANKS)
                dve.wait_ge(max_filled[bank], MAX_UNITS * j + turn + 1)
                if tile == 0 and u == 0 and due(k):
                    dve.wait_ge(neg_max_ready, k)
                nc.vector.tensor_reduce(half_max[:, a, tile, half:half + 1], max_ps[:, bank, :], AX_X,
                                        ALU.max).then_inc(max_read[bank], 1)

            def read(st, s):
                kind, i = st.extra(s)
                g = st.ordinal(s)
                if kind == "shift":
                    k = PAIRS * st.shifted(i)[0] + i
                    dve.wait_ge(extra_filled, g + 1)
                    if due(k):
                        dve.wait_ge(shift_moved, MOVE * 2 * k)
                    turned = extra_ps[0:2 * TILES, 0:P]
                    nc.vector.tensor_scalar(shift_rows[:, 0, :], turned, 1.0 / SHIFT, None,
                                            ALU.mult).then_inc(shift_step, 1)
                    dve.wait_ge(shift_step, 2 * k + 1)
                    nc.vector.scalar_tensor_tensor(out=shift_rows[:, 1, :], in0=turned, scalar=1.0 / SHIFT,
                                                   in1=shift_rows[:, 0, :], op0=ALU.mult,
                                                   op1=ALU.subtract).then_inc(shift_step, 1)
                    dve.wait_ge(shift_step, 2 * k + 2)
                    dve.sem_inc(extra_freed, 1)
                elif kind == "mean":
                    j = st.b + 2
                    dve.wait_ge(extra_filled, g + 1)
                    nc.vector.tensor_tensor(mu_off[:, :], chan_stats[:, :, 0], extra_ps[:, 0:2],
                                            ALU.subtract).then_inc(stats_step, 1)
                    nc.vector.tensor_scalar(neg_mu[:, :], extra_ps[:, 0:2], -1.0, None,
                                            ALU.mult).then_inc(extra_freed, 1)
                    dve.wait_ge(stats_step, STATS * j + 7)
                    nc.vector.tensor_tensor(mu_off2[:, :], mu_off[:, :], mu_off[:, :],
                                            ALU.mult).then_inc(stats_step, 1)
                    dve.wait_ge(stats_step, STATS * j + 8)
                    nc.vector.tensor_tensor(chan_var[:, :], chan_stats[:, :, 1], mu_off2[:, :],
                                            ALU.add).then_inc(stats_step, 1)
                elif kind == "var":
                    dve.wait_ge(extra_filled, g + 1)
                    nc.vector.tensor_scalar(var_eps[:, :], extra_ps[:, 0:2], EPS, None,
                                            ALU.add).then_inc(extra_freed, 1)
                elif kind == "qk":
                    t, half = divmod(i, 2)
                    n = slice(HALF * half, HALF * (half + 1))
                    dve.wait_ge(qk_hi_ready, 6 * st.made(i)[0] + i + 1)
                    nc.vector.tensor_tensor(qk_lo[:, t, n], extra_ps[:, :], qk_hi[:, t, n],
                                            ALU.subtract).then_inc(extra_freed, 1)

            def add_quad(j, q, a, half):
                n = slice(HALF * half, HALF * (half + 1))
                dve.wait_ge(pairs_added, 4 * (SLOTS // QUAD * j + q) + 3 + a)
                second = prob_pairs[:, a, (2 * q + 1) % PAIR_RING, n]
                nc.vector.tensor_tensor(second, prob_pairs[:, a, 2 * q % PAIR_RING, n], second,
                                        ALU.add).then_inc(quads_added, 1)

            def step(st):
                for s in range(SLOTS):
                    for u in range(SCORE_UNITS):
                        for half in range(HALVES):
                            for j, par, q in st.due(s, QUAD_ADDED + half, QUAD):
                                if u % 2 == 1:
                                    add_quad(j, q, u // 2, half)
                        if u == 0 and s > 0 and st.extra(s - 1) is not None:
                            read(st, s - 1)
                        if st.take_stats and (s, u) in STATS_AT:
                            half_statistics(st, STATS_AT.index((s, u)))
                        if st.take_stats and (s, u) == AGGREGATE_AT:
                            statistics(st)
                        if st.maxed(s) is not None:
                            row_max(st, s, u)
                    for j, par, p in st.due(s, INVERTED, TILES):
                        k = PAIRS * j + p
                        dve.wait_ge(sums_spread_out, MOVE * (k + 1))
                        if due(k):
                            dve.wait_ge(inv_gathered, MOVE * k)
                        nc.vector.reciprocal(inv_spread[:, :], sums_spread[:, :]).then_inc(inverted, 1)
                    if st.maxed(s) is not None and st.maxed(s)[2] % TILES == TILES - 1:
                        j, par, at = st.maxed(s)
                        for bank in range(MAX_BANKS):
                            dve.wait_ge(max_read[bank], MAX_UNITS * j
                                        + (SCORE_UNITS * (at + 1) - bank + MAX_BANKS - 1) // MAX_BANKS)
                        nc.vector.tensor_reduce(neg_max[:, :],
                                                half_max[:, :, :, :].rearrange("p a t h -> p (a t) h"),
                                                AX_X, ALU.max, negate=True).then_inc(neg_max_ready, 1)

            run_steps(dve, step)




def u_bank(s, u):
    return (SCORE_UNITS * s + u) % SCORE_BANKS


def kernel(x, L0_conv_qkv_w, L0_conv_proj_w, L0_conv_proj_b):
    import concourse.bacc as bacc
    from concourse.bass_utils import run_bass_kernel_spmd

    channel = np.arange(C) // GROUP
    paired = np.arange(C).reshape(PAIRS, 2, D).transpose(0, 2, 1).reshape(C)
    order = np.concatenate([paired, C + paired, np.arange(2 * C, 3 * C)])
    arrays = {
        "x": np.ascontiguousarray(x).reshape(BATCH, C, N),
        "qkv_wT": np.ascontiguousarray(np.asarray(L0_conv_qkv_w).T[:, order]),
        "proj_wT": np.ascontiguousarray(np.asarray(L0_conv_proj_w).T),
        "proj_b": np.ascontiguousarray(np.asarray(L0_conv_proj_b).reshape(2, OM).T),
        "group_mean": np.where(channel[:, None] == channel[None, :], np.float32(1.0 / GROUP), np.float32(0.0)),
        "identity": np.eye(P, dtype=np.float32),
    }
    nc = bacc.Bacc("TRN2", target_bir_lowering=False, num_devices=1)
    ins = [nc.dram_tensor(name, a.shape, mybir.dt.from_np(a.dtype), kind="ExternalInput").ap()
           for name, a in arrays.items()]
    out = nc.dram_tensor("out", (BATCH, C, N), F32, kind="ExternalOutput").ap()
    group_norm_attention(nc, *ins, out)
    r = run_bass_kernel_spmd(nc, [arrays], core_ids=[0])
    return r.results[0]["out"].reshape(BATCH, C, H, W)
```
